# Optimizing a Trainium2 kernel written in Bass

```python
import numpy as np
import jax
import jax.numpy as jnp

def _softmax(x, axis=-1):
    return jax.nn.softmax(x, axis=axis)

def _gelu(x):
    return jax.nn.gelu(x, approximate=True)

def _silu(x):
    return jax.nn.silu(x)

def _sigmoid(x):
    return jax.nn.sigmoid(x)

def _layernorm(x, axis=-1, eps=1e-05):
    m = jnp.mean(x, axis=axis, keepdims=True)
    v = jnp.var(x, axis=axis, keepdims=True)
    return (x - m) / jnp.sqrt(v + eps)

def _scatter_add(tgt, idx, src, axis=0):
    return tgt.at[idx].add(src)

def _segment_sum(src, seg, n):
    return jax.ops.segment_sum(src, seg, n)
kernel_name = 'mk_gnn_resnorm_d2_gnn_r32_2d070c'

def setup_inputs(seed: int=0):
    np.random.seed(seed)
    _w = jnp.asarray

    def _rec_inputs():
        import jax
        import jax.numpy as jnp
        _gk = jax.random.key(seed)
        x = -0.0005121 + 1.001 * jax.random.normal(jax.random.fold_in(_gk, 1), (3125, 64), jnp.float32)
        _s = jax.random.randint(jax.random.fold_in(_gk, 2), (25000,), 0, 3125, jnp.int32)
        _d = jax.random.randint(jax.random.fold_in(_gk, 3), (25000,), 0, 3125, jnp.int32)
        _loop = jnp.arange(3125, dtype=jnp.int32)
        src = jnp.concatenate([_s, _d, _loop])
        dst = jnp.concatenate([_d, _s, _loop])
        _o = jnp.argsort(dst, stable=True)
        src = src[_o]
        dst = dst[_o]
        edge_attr_3 = jax.random.uniform(jax.random.fold_in(_gk, 12), (53125, 3), jnp.float32, 0.0, 0.999999)
        edge_attr_64 = -8.16379e-05 + 0.999858 * jax.random.normal(jax.random.fold_in(_gk, 13), (53125, 64), jnp.float32)
        return (x, src, dst, edge_attr_3, edge_attr_64)
    x, src, dst, edge_attr_3, edge_attr_64 = _rec_inputs()

    def _L0_gnn_setup():
        import jax, jax.numpy as jnp
        import numpy as np
        N, E = (50000, 25000)
        C_IN, C_OUT, DIM, K = (64, 64, 3, 2)
        EPS = 1e-05

        def _spline_basis(edge_attr):
            D = edge_attr.shape[1]
            v = edge_attr * (K - 1)
            k0 = jnp.floor(v)
            frac = v - k0
            k0 = k0.astype(jnp.int32)
            bits = np.stack(np.unravel_index(np.arange(2 ** D), (2,) * D), axis=-1).astype(np.int32)
            bits_f = jnp.asarray(bits, dtype=edge_attr.dtype)
            w = jnp.where(bits_f[None] > 0, frac[:, None, :], 1.0 - frac[:, None, :])
            weights = jnp.prod(w, axis=-1)
            idx_d = jnp.clip(k0[:, None, :] + bits[None], 0, K - 1)
            radix = jnp.asarray(K ** np.arange(D), dtype=jnp.int32)
            idx = jnp.sum(idx_d * radix, axis=-1)
            return (weights, idx)
        key = jax.random.key(seed)
        k1, k2, k3, k4, k5 = jax.random.split(key, 5)
        x = jax.random.normal(k1, (N, C_IN), dtype=jnp.float32)
        edge_index = jax.random.randint(k2, (2, E), 0, N, dtype=jnp.int32)
        edge_attr = jax.random.uniform(k3, (E, DIM), dtype=jnp.float32)
        W = jax.random.normal(k4, (K ** DIM, C_IN, C_OUT), dtype=jnp.float32) * 0.05
        root = jax.random.normal(k5, (C_IN, C_OUT), dtype=jnp.float32) * 0.05
        gamma = jnp.ones((C_OUT,), dtype=jnp.float32)
        beta = jnp.zeros((C_OUT,), dtype=jnp.float32)
        return {'x': x, 'edge_attr': edge_attr, 'W': W, 'root': root, 'gamma': gamma, 'beta': beta, 'edge_index': edge_index}
    _L0_gnn_all = _L0_gnn_setup()
    _L0_gnn_in = {k: v for k, v in _L0_gnn_all.items() if k in ('W', 'root', 'gamma', 'beta')}
    del _L0_gnn_all

    def _L1_gnn_setup():
        import jax, jax.numpy as jnp
        import numpy as np
        N_NODES = 3125
        N_EDGES = 50000
        EMB = 64
        BN_EPS = 1e-05
        key = jax.random.key(seed)
        ks = jax.random.split(key, 8)
        node_feats = jax.random.normal(ks[0], (N_NODES, EMB), dtype=jnp.float32)
        edge_feats = jax.random.normal(ks[1], (N_EDGES, EMB), dtype=jnp.float32)
        src = jax.random.randint(ks[2], (N_EDGES,), 0, N_NODES, dtype=jnp.int32)
        dst = jax.random.randint(ks[3], (N_EDGES,), 0, N_NODES, dtype=jnp.int32)
        lim1 = 1.0 / np.sqrt(EMB)
        lim2 = 1.0 / np.sqrt(2 * EMB)
        W1 = jax.random.uniform(ks[4], (EMB, 2 * EMB), minval=-lim1, maxval=lim1, dtype=jnp.float32)
        b1 = jax.random.uniform(ks[5], (2 * EMB,), minval=-lim1, maxval=lim1, dtype=jnp.float32)
        W2 = jax.random.uniform(ks[6], (2 * EMB, EMB), minval=-lim2, maxval=lim2, dtype=jnp.float32)
        b2 = jax.random.uniform(ks[7], (EMB,), minval=-lim2, maxval=lim2, dtype=jnp.float32)
        bn_gamma = jnp.ones((EMB,), dtype=jnp.float32)
        bn_beta = jnp.zeros((EMB,), dtype=jnp.float32)
        return {'node_feats': node_feats, 'edge_feats': edge_feats, 'src': src, 'dst': dst, 'W1': W1, 'b1': b1, 'W2': W2, 'b2': b2, 'bn_gamma': bn_gamma, 'bn_beta': bn_beta}
    _L1_gnn_all = _L1_gnn_setup()
    _L1_gnn_in = {k: v for k, v in _L1_gnn_all.items() if k in ('W1', 'b1', 'W2', 'b2', 'bn_gamma', 'bn_beta')}
    del _L1_gnn_all
    return {'x': x, 'src': src, 'dst': dst, 'edge_attr_3': edge_attr_3, 'edge_attr_64': edge_attr_64, 'L0_gnn_W': _L0_gnn_in['W'], 'L0_gnn_root': _L0_gnn_in['root'], 'L0_gnn_gamma': _L0_gnn_in['gamma'], 'L0_gnn_beta': _L0_gnn_in['beta'], 'L1_gnn_W1': _L1_gnn_in['W1'], 'L1_gnn_b1': _L1_gnn_in['b1'], 'L1_gnn_W2': _L1_gnn_in['W2'], 'L1_gnn_b2': _L1_gnn_in['b2'], 'L1_gnn_bn_gamma': _L1_gnn_in['bn_gamma'], 'L1_gnn_bn_beta': _L1_gnn_in['bn_beta']}

def reference(x, src, dst, edge_attr_3, edge_attr_64, L0_gnn_W, L0_gnn_root, L0_gnn_gamma, L0_gnn_beta, L1_gnn_W1, L1_gnn_b1, L1_gnn_W2, L1_gnn_b2, L1_gnn_bn_gamma, L1_gnn_bn_beta):
    import jax
    import jax.numpy as jnp

    def _L0_gnn_ref(x, edge_attr, W, root, gamma, beta, edge_index):
        import jax, jax.numpy as jnp
        import numpy as np
        N, E = (50000, 25000)
        C_IN, C_OUT, DIM, K = (64, 64, 3, 2)
        EPS = 1e-05

        def _spline_basis(edge_attr):
            D = edge_attr.shape[1]
            v = edge_attr * (K - 1)
            k0 = jnp.floor(v)
            frac = v - k0
            k0 = k0.astype(jnp.int32)
            bits = np.stack(np.unravel_index(np.arange(2 ** D), (2,) * D), axis=-1).astype(np.int32)
            bits_f = jnp.asarray(bits, dtype=edge_attr.dtype)
            w = jnp.where(bits_f[None] > 0, frac[:, None, :], 1.0 - frac[:, None, :])
            weights = jnp.prod(w, axis=-1)
            idx_d = jnp.clip(k0[:, None, :] + bits[None], 0, K - 1)
            radix = jnp.asarray(K ** np.arange(D), dtype=jnp.int32)
            idx = jnp.sum(idx_d * radix, axis=-1)
            return (weights, idx)
        src, dst = (edge_index[0], edge_index[1])
        Etot = edge_attr.shape[0]
        S = W.shape[0]
        weights, idx = _spline_basis(edge_attr)
        B = jnp.zeros((Etot, S), dtype=x.dtype).at[jnp.arange(Etot)[:, None], idx].add(weights)
        xj = x[src]
        z = (B[:, :, None] * xj[:, None, :]).reshape(Etot, S * x.shape[1])
        msg = z @ W.reshape(S * x.shape[1], W.shape[2])
        agg = jax.ops.segment_sum(msg, dst, num_segments=x.shape[0])
        cnt = jax.ops.segment_sum(jnp.ones((Etot,), dtype=x.dtype), dst, num_segments=x.shape[0])
        out = agg / jnp.maximum(cnt, 1.0)[:, None] + x @ root
        mean = jnp.mean(out, axis=0)
        var = jnp.var(out, axis=0)
        y = (out - mean) * jax.lax.rsqrt(var + EPS) * gamma + beta
        return jax.nn.elu(y)

    def _L1_gnn_ref(node_feats, edge_feats, src, dst, W1, b1, W2, b2, bn_gamma, bn_beta):
        import jax, jax.numpy as jnp
        import numpy as np
        N_NODES = 3125
        N_EDGES = 50000
        EMB = 64
        BN_EPS = 1e-05
        n_nodes = node_feats.shape[0]
        msg = node_feats[src] + edge_feats
        agg = jax.ops.segment_sum(msg, dst, num_segments=n_nodes)
        h = jax.nn.relu(agg @ W1 + b1) @ W2 + b2
        mean = jnp.mean(h, axis=0)
        var = jnp.mean(jnp.square(h - mean), axis=0)
        h = (h - mean) * jax.lax.rsqrt(var + BN_EPS) * bn_gamma + bn_beta
        return h
    edge_index = jnp.stack([src, dst])
    x = _layernorm(x + _L0_gnn_ref(x, edge_attr_3, L0_gnn_W, L0_gnn_root, L0_gnn_gamma, L0_gnn_beta, edge_index), axis=-1)
    x = _layernorm(x + _L1_gnn_ref(x, edge_attr_64, src, dst, L1_gnn_W1, L1_gnn_b1, L1_gnn_W2, L1_gnn_b2, L1_gnn_bn_gamma, L1_gnn_bn_beta), axis=-1)
    return x

_drawn_inputs = setup_inputs


def setup_inputs(seed=0):
    import zlib

    import numpy as np

    out = dict(_drawn_inputs(seed))
    spreads = {'L0_gnn_gamma': (1.0, 0.2),
     'L0_gnn_beta': (0.0, 0.1),
     'L1_gnn_bn_gamma': (1.0, 0.2),
     'L1_gnn_bn_beta': (0.0, 0.1)}
    factors = {'L1_gnn_b1': 3.927, 'L1_gnn_b2': 8.0}
    for name, (base, spread) in spreads.items():
        noise = np.random.default_rng([zlib.crc32(name.encode()), seed]).standard_normal(out[name].shape)
        drawn = base * np.exp(spread * noise) if base else spread * noise
        out[name] = jnp.asarray(drawn.astype(out[name].dtype))
    for name, factor in factors.items():
        out[name] = (out[name] * factor).astype(out[name].dtype)
    return out
```

```python
from contextlib import ExitStack

import concourse.bass as bass
from concourse import mybir

F32 = mybir.dt.float32
I32 = mybir.dt.int32
ALU = mybir.AluOpType
ACT = mybir.ActivationFunctionType
AX = mybir.AxisListType


def gnn_two_layers(nc, x, src, dst, ea3, ea64, wk_d, root_d, gamma0, beta0,
                   w1_d, b1_d, w2_d, b2_d, gamma1, beta1, out):
    P = 128
    N, C = x.shape
    E = src.shape[0]
    NK = wk_d.shape[0]
    HID = w1_d.shape[1]
    D = ea3.shape[1]
    SLOTS = 4
    CH = 8
    T = -(-E // (P * CH * SLOTS)) * CH * SLOTS
    NCH = T // CH
    AHEAD = SLOTS
    SUP = 2
    WPC = CH // SUP
    WIN = 24
    KIN = NK + 1
    ZW = KIN * WIN
    RW = WPC * WIN
    NR = -(-(N + WIN) // RW)
    NPAD = NR * RW
    PN = 125
    NT = N // PN
    TPB = 7
    NB = -(-NT // TPB)
    FULL = E // P
    REST = E - FULL * P
    BLK = -(-T // P)
    LASTROWS = FULL - (BLK - 1) * P
    TB = T - (BLK - 1) * P
    NOWHERE = -8192.0
    EPS = 1e-5
    assert N == PN * NT and NB <= 4 and BLK == 4 and D == 3 and NK == 8
    assert 0 <= LASTROWS < TB and P == 2 * C and HID == P and FULL == T - 1

    ctx = ExitStack()
    with ctx:
        def sb(name, shape, dt=F32):
            return ctx.enter_context(nc.sbuf_tensor(name, shape, dt))

        def sem(name):
            return ctx.enter_context(nc.semaphore(name))

        src_rows = sb("src_rows", [P, BLK, P], I32)
        dst_rows = sb("dst_rows", [P, BLK, P], I32)
        src_col = sb("src_col", [P, T + AHEAD * CH], I32)
        idx = sb("idx", [P, SLOTS, CH], I32)
        dst_col = sb("dst_col", [P, T])
        rel = sb("rel", [P, T + CH])
        real = sb("real", [P, T])
        missed = sb("missed", [P, T])
        missed2 = sb("missed2", [P, T])
        missed_dst = sb("missed_dst", [P, T])
        missed_row = sb("missed_row", [P, 1])
        missed_any = sb("missed_any", [1, 1], I32)
        base = sb("base", [1, T // SUP], I32)
        basis = sb("basis", [P, T + CH, KIN])
        hot = sb("hot", [P, T + CH, WIN])
        place = hot[:, :, :].rearrange("p t w -> p (t w)")
        sizes = [BLK * P * D, BLK * P, BLK * P, D * T * 2, T * 4]
        ends = [sum(sizes[:n + 1]) for n in range(len(sizes))]
        ea3_rows, src_rows_f, dst_rows_f, w_lohi, w_pair = (place[:, e - n:e] for n, e in zip(sizes, ends))
        assert ends[-1] <= (T + CH) * WIN and N <= (T + CH) * WIN
        ea3_rows = ea3_rows.rearrange("p (b e d) -> p b e d", b=BLK, e=P)
        src_rows_f = src_rows_f.rearrange("p (b e) -> p b e", b=BLK)
        dst_rows_f = dst_rows_f.rearrange("p (b e) -> p b e", b=BLK)
        w_lohi = w_lohi.rearrange("p (d t s) -> p d t s", d=D, s=2)
        w_pair = w_pair.rearrange("p (t s) -> p t s", s=4)
        hid = place[:, 0:N]
        whot = sb("whot", [P, 2, CH, ZW])
        rows = sb("rows", [P, SLOTS, CH, P])
        z_sb = sb("z_sb", [P, 2, WPC, KIN, WIN])
        agg0 = sb("agg0", [C + 1, NPAD])
        agg1 = sb("agg1", [P, NPAD])
        x_nm = sb("x_nm", [PN, NT, C])
        xt = sb("xt", [C, N])
        xroot = sb("xroot", [PN, NT, C])
        ident = sb("ident", [P, P])
        ones = sb("ones", [P, P])
        iota_i = sb("iota_i", [P, RW], I32)
        iota_f = sb("iota_f", [P, RW])
        wk = sb("wk", [C, NK, C])
        root = sb("root", [C, C])
        w1 = sb("w1", [P, HID])
        w2 = sb("w2", [HID, C])
        b1 = sb("b1", [HID, 1])
        vecs = sb("vecs", [PN, 5, C])
        h = sb("h", [PN, NT, C])
        sq = sb("sq", [PN, NT, C])
        x1 = sb("x1", [PN, NT, C])
        res = sb("res", [PN, NT, C])
        inv_cnt = sb("inv_cnt", [PN, NT])
        mean = sb("mean", [PN, C])
        var = sb("var", [PN, C])
        std = sb("std", [PN, C])
        scale = sb("scale", [PN, C])
        ln_sum = sb("ln_sum", [PN, NT])
        ln_mean = sb("ln_mean", [PN, NT])
        ln_var = sb("ln_var", [PN, NT])
        ln_std = sb("ln_std", [PN, NT])
        ln_rstd = sb("ln_rstd", [PN, NT])
        fb_idx = sb("fb_idx", [P, 1], I32)
        fb_rel = sb("fb_rel", [P, 2])
        fb_hot = sb("fb_hot", [P, RW])
        fb_whot = sb("fb_whot", [P, WPC, KIN, WIN])
        x1_dram = nc.dram_tensor("x1_scratch", (N, C), F32).ap()

        z_ps = ctx.enter_context(nc.psum_tensor("z_ps", [P, 4, 512], F32))
        t_ps = ctx.enter_context(nc.psum_tensor("t_ps", [P, 2, 512], F32))
        m_ps = ctx.enter_context(nc.psum_tensor("m_ps", [P, 2, 512], F32))

        pads_set = sem("pads_set")
        src_loaded, dst_loaded, ea3_loaded = sem("src_loaded"), sem("dst_loaded"), sem("ea3_loaded")
        x_loaded, weights_loaded, vecs_loaded = sem("x_loaded"), sem("weights_loaded"), sem("vecs_loaded")
        pool_step = sem("pool_step")
        ident_ready, iota_ready, ones_ready = sem("ident_ready"), sem("iota_ready"), sem("ones_ready")
        src_f_ready, dst_f_ready = sem("src_f_ready"), sem("dst_f_ready")
        src_turned, dst_turned, ea3_turned = sem("src_turned"), sem("dst_turned"), sem("ea3_turned")
        src_col_ready, dst_col_ready, basis_in = sem("src_col_ready"), sem("dst_col_ready"), sem("basis_in")
        base_spread, missed_ready, missed_summed, flag_ready = (
            sem("base_spread"), sem("missed_ready"), sem("missed_summed"), sem("flag_ready"))
        xt_turned, xt_ready, xroot_done, xroot_ready = (
            sem("xt_turned"), sem("xt_ready"), sem("xroot_done"), sem("xroot_ready"))
        idx_ready = sem("idx_ready")
        begun = sem("begun")
        gathered = [sem(f"gathered{s}") for s in range(SLOTS)]
        summed = sem("summed")
        hot_ready, whot_ready = sem("hot_ready"), sem("whot_ready")
        z_free, zsb_ready = sem("z_free"), sem("zsb_ready")
        t_ready, t_free = sem("t_ready"), sem("t_free")
        added0, added1 = sem("added0"), sem("added1")
        agg0_done, agg1_done = sem("agg0_done"), sem("agg1_done")
        ea_rest_loaded = sem("ea_rest_loaded")
        ea_loaded = [sem(f"ea_loaded{s}") for s in range(SLOTS)]
        a_free = sem("a_free")
        fb_fetched, fb_idx_ready, fb_ea = sem("fb_fetched"), sem("fb_idx_ready"), sem("fb_ea")
        fb_w, fb_z, fb_zsb, fb_t, fb_step = sem("fb_w"), sem("fb_z"), sem("fb_zsb"), sem("fb_t"), sem("fb_step")
        fb_added = sem("fb_added")
        turned0 = sem("turned0")
        h_ready = [sem("h0_ready"), sem("h1_ready")]
        sums_ready = [sem("sums0_ready"), sem("sums1_ready")]
        centred = [sem("centred0"), sem("centred1")]
        squared = [sem("squared0"), sem("squared1")]
        vars_ready = [sem("vars0_ready"), sem("vars1_ready")]
        var_ready = [sem("var0_ready"), sem("var1_ready")]
        std_ready = [sem("std0_ready"), sem("std1_ready")]
        y_ready, exp_ready = sem("y_ready"), sem("exp_ready")
        ln_centred = [sem("ln_centred0"), sem("ln_centred1")]
        ln_squared = [sem("ln_squared0"), sem("ln_squared1")]
        ln_var_ready = [sem("ln_var0_ready"), sem("ln_var1_ready")]
        ln_std_ready = [sem("ln_std0_ready"), sem("ln_std1_ready")]
        x1_ready, x1_stored, out_ready, out_stored = (
            sem("x1_ready"), sem("x1_stored"), sem("out_ready"), sem("out_stored"))
        hid_ps_ready, hid_ready, h1_ps_ready = sem("hid_ps_ready"), sem("hid_ready"), sem("h1_ps_ready")
        dve_step = sem("dve_step")

        block = ctx.enter_context(nc.Block())

        def node_major(a):
            return a.rearrange("(t p) c -> p t c", p=PN)

        def bank_tiles(b):
            return range(b * TPB, min((b + 1) * TPB, NT))

        ea64_full = ea64[0:FULL * P, :].rearrange("(t p) c -> p t c", p=P)
        MMCOL = 450
        assert N % MMCOL != 0 or True
        HCH = [(a, min(a + MMCOL, N)) for a in range(0, N, MMCOL)]

        @block.sync
        def _(sp):
            sp.wait_ge(pads_set, 3)

            def load_rows(tile, d, loaded, per):
                lead = (BLK - 1) * P * P
                view = d if per == 1 else d.rearrange("e d -> (e d)")
                sp.dma_start(tile[:, 0:BLK - 1], view[0:lead * per].rearrange(
                    "(b r k) -> r b k", b=BLK - 1, r=P)).then_inc(loaded, 16)
                sp.dma_start(tile[0:LASTROWS, BLK - 1], view[lead * per:FULL * P * per].rearrange(
                    "(r k) -> r k", r=LASTROWS)).then_inc(loaded, 16)
                sp.dma_start(tile[LASTROWS:LASTROWS + 1, BLK - 1, 0:REST * per],
                             view[FULL * P * per:E * per].rearrange("(r k) -> r k", r=1)).then_inc(loaded, 16)

            load_rows(src_rows, src, src_loaded, 1)
            load_rows(dst_rows, dst, dst_loaded, 1)
            load_rows(ea3_rows[:, :, :, :].rearrange("p b e d -> p b (e d)"), ea3, ea3_loaded, D)
            sp.dma_start(x_nm[:, :, :], node_major(x)).then_inc(x_loaded, 16)
            sp.dma_start(root[:, :], root_d).then_inc(weights_loaded, 16)
            sp.dma_start(wk[:, :, :], wk_d.rearrange("k i o -> i k o")).then_inc(weights_loaded, 16)
            sp.dma_start(w1[0:C, :], w1_d).then_inc(weights_loaded, 16)
            sp.dma_start(w1[C:P, :], w1_d).then_inc(weights_loaded, 16)
            sp.dma_start(w2[:, :], w2_d).then_inc(weights_loaded, 16)
            sp.dma_start(b1[:, :], b1_d.rearrange("(p a) -> p a", a=1)).then_inc(weights_loaded, 16)
            for n, v in enumerate((gamma0, beta0, b2_d, gamma1, beta1)):
                sp.dma_start(vecs[:, n, :], v.rearrange("(a c) -> a c", a=1).to_broadcast([PN, C])
                             ).then_inc(vecs_loaded, 16)

            def load_ea(c, s):
                sp.wait_ge(summed, c + (NCH + 1))
                sp.dma_start(rows[:, s, :, C:P], ea64_full[:, bass.ds(c * CH, CH), :]).then_inc(ea_loaded[s], 16)

            sp.wait_ge(agg0_done, 2)
            with sp.Fori(0, NCH // SLOTS - 1) as i:
                for s in range(SLOTS):
                    load_ea(i * SLOTS + s, s)
            for s in range(SLOTS - 1):
                load_ea(NCH - SLOTS + s, s)
            sp.wait_ge(summed, NCH + NCH)
            sp.dma_start(rows[0:REST, SLOTS - 1, CH - 1, C:P], ea64[FULL * P:E, :]).then_inc(ea_rest_loaded, 16)
            sp.wait_ge(ea_rest_loaded, 16)
            sp.dma_start(rows[:, SLOTS - 1, 0:CH - 1, C:P], ea64_full[:, FULL - CH + 1:FULL, :]).then_inc(
                ea_loaded[SLOTS - 1], 16)

            sp.wait_ge(flag_ready, 1)
            flag = sp.value_load(missed_any[0:1, 0:1], min_val=0, max_val=1 << 20)
            with sp.If(flag > 0):
                sp.wait_ge(agg1_done, 1)
                with sp.Fori(0, FULL) as t:
                    sp.wait_ge(fb_added, (T + t) * NR + 1)
                    sp.dma_start(rows[:, 0, 0, C:P], ea64[bass.ds(t * P, P), :]).then_inc(fb_ea, 16)
                sp.wait_ge(fb_added, (T + FULL) * NR + 1)
                sp.dma_start(rows[0:REST, 0, 0, C:P], ea64[FULL * P:E, :]).then_inc(fb_ea, 16)

            for b in range(NB):
                ts = bank_tiles(b)
                sp.wait_ge(out_ready, b + 1)
                sp.dma_start(node_major(out)[:, ts[0]:ts[-1] + 1, :],
                             res[:, ts[0]:ts[-1] + 1, :]).then_inc(out_stored, 16)
            sp.wait_ge(out_stored, 16 * NB)

        @block.gpsimd
        def _(pool):
            nc.gpsimd.memset(ident[:, :], 0.0).then_inc(pool_step, 1)
            nc.gpsimd.iota(iota_i[:, :], pattern=[[1, RW]], base=0, channel_multiplier=0).then_inc(iota_ready, 1)
            pool.wait_ge(pool_step, 1)
            nc.gpsimd.affine_select(out=ident[:, :], in_=ident[:, :], compare_op=ALU.not_equal, fill=1.0,
                                    base=0, pattern=[[-1, P]], channel_multiplier=1).then_inc(ident_ready, 1)

            def gather(table, chunks_before):
                with pool.Fori(0, NCH // SLOTS) as i:
                    for s in range(SLOTS):
                        c = i * SLOTS + (s + chunks_before + 1)
                        pool.wait_ge(idx_ready, c)
                        pool.wait_ge(summed, c)
                        pool.sem_inc(begun, 1)
                        for t in range(CH):
                            pool.indirect_dma_start(
                                rows[:, s, t, 0:C], None, table,
                                bass.IndirectOffsetOnAxis(ap=idx[:, s, t:t + 1], axis=0)).then_inc(gathered[s], 16)

            def gather_missed(table, flag, done, tiles_before):
                with pool.If(flag > 0):
                    pool.wait_ge(done, 1)
                    with pool.Fori(0, T) as t:
                        pool.wait_ge(fb_idx_ready, t + (tiles_before + 1))
                        pool.wait_ge(fb_added, (t + tiles_before) * NR + 1)
                        pool.sem_inc(begun, 1)
                        pool.indirect_dma_start(
                            rows[:, 0, 0, 0:C], None, table,
                            bass.IndirectOffsetOnAxis(ap=fb_idx[:, 0:1], axis=0)).then_inc(fb_fetched, 16)

            gather(x, 0)
            pool.wait_ge(flag_ready, 1)
            flag = pool.value_load(missed_any[0:1, 0:1], min_val=0, max_val=1 << 20)
            gather_missed(x, flag, agg0_done, 0)
            pool.wait_ge(x1_stored, 16 * NB)
            gather(x1_dram, NCH)
            gather_missed(x1_dram, flag, agg1_done, T)

        @block.tensor
        def _(pe):
            pe.wait_ge(ident_ready, 1)

            def turn_rows(dstp, rows_of, turned):
                for b in range(BLK):
                    n = P if b < BLK - 1 else TB
                    last = nc.tensor.transpose(dstp[:, b * P:b * P + n], rows_of(b)[0:n, :], ident[0:n, 0:n])
                last.then_inc(turned, 1)

            pe.wait_ge(src_f_ready, 1)
            turn_rows(m_ps[:, 0, :], lambda b: src_rows_f[:, b, :], src_turned)
            pe.wait_ge(dst_f_ready, 1)
            turn_rows(m_ps[:, 1, :], lambda b: dst_rows_f[:, b, :], dst_turned)
            pe.wait_ge(ones_ready, 1)
            pe.wait_ge(src_col_ready, 1)
            pe.wait_ge(dst_col_ready, 1)
            nc.tensor.matmul(m_ps[:, 0, 0:T // SUP], ones[0:1, :], dst_col[0:1, 0:T:SUP],
                             start=True, stop=True).then_inc(base_spread, 1)
            pe.wait_ge(ea3_loaded, 48)
            for d in range(D):
                turn_rows(z_ps[:, d, :], lambda b: ea3_rows[:, b, :, d], ea3_turned)
            pe.wait_ge(missed_ready, 1)
            nc.tensor.matmul(m_ps[0:1, 1, 0:1], missed_row[:, 0:1], ones[:, 0:1],
                             start=True, stop=True).then_inc(missed_summed, 1)
            pe.wait_ge(x_loaded, 16)
            for g in range(-(-NT // 4)):
                if g >= 2:
                    pe.wait_ge(xt_ready, g - 1)
                for j in range(4 * g, min(4 * g + 4, NT)):
                    last = nc.tensor.transpose(t_ps[0:C, g % 2, (j % 4) * PN:(j % 4 + 1) * PN],
                                               x_nm[:, j, :], ident[0:PN, 0:PN])
                last.then_inc(xt_turned, 1)
            pe.wait_ge(xt_ready, -(-NT // 4))
            pe.wait_ge(basis_in, 1)
            pe.wait_ge(weights_loaded, 96)
            for b in range(NB):
                for j in bank_tiles(b):
                    last = nc.tensor.matmul(z_ps[0:PN, b, (j % TPB) * C:(j % TPB + 1) * C],
                                            xt[:, j * PN:(j + 1) * PN], root[:, :], start=True, stop=True)
            last.then_inc(xroot_done, 1)
            pe.wait_ge(xroot_ready, 1)

            def z_out(zs, w):
                return z_ps[:, 2 * zs + w // 2, (w % 2) * ZW:(w % 2 + 1) * ZW]

            def through_kernels(zs, ts, ready):
                for k in range(NK):
                    nc.tensor.matmul(t_ps[0:C, ts, 0:RW], wk[:, k, :], z_sb[0:C, zs, :, k, :],
                                     start=(k == 0), stop=(k == NK - 1))
                nc.tensor.matmul(t_ps[C:C + 1, ts, 0:RW], ones[C:C + 1, 0:1], z_sb[C:C + 1, zs, :, NK, :],
                                 start=True, stop=True).then_inc(ready, 1)

            with pe.Fori(0, NCH // SLOTS) as i:
                for s in range(SLOTS):
                    c = i * SLOTS + s
                    zs = s % 2
                    pe.wait_ge(gathered[s], i * (CH * 16) + CH * 16)
                    pe.wait_ge(whot_ready, c + 1)
                    pe.wait_ge(z_free, c + 1)
                    for t in range(CH):
                        last = nc.tensor.matmul(z_out(zs, t // SUP), rows[:, s, t, :], whot[:, zs, t, :],
                                                start=(t % SUP == 0), stop=(t % SUP == SUP - 1))
                    last.then_inc(summed, 1)
                    pe.wait_ge(weights_loaded, 96)
                    pe.wait_ge(zsb_ready, c + 1)
                    pe.wait_ge(t_free, c + 1)
                    through_kernels(zs, zs, t_ready)

            pe.wait_ge(flag_ready, 1)
            flag = pe.value_load(missed_any[0:1, 0:1], min_val=0, max_val=1 << 20)
            with pe.If(flag > 0):
                with pe.Fori(0, T) as t:
                    with pe.Fori(0, NR) as r:
                        n = t * NR + r
                        pe.wait_ge(fb_fetched, t * 16 + 16)
                        pe.wait_ge(fb_w, n + 1)
                        for w in range(WPC):
                            last = nc.tensor.matmul(z_out(0, w), rows[:, 0, 0, :],
                                                    fb_whot[:, w, :, :], start=True, stop=True)
                        last.then_inc(fb_z, 1)
                        pe.wait_ge(weights_loaded, 96)
                        pe.wait_ge(fb_zsb, n + 1)
                        through_kernels(0, 0, fb_t)

            pe.wait_ge(agg0_done, 2)
            for b in range(NB):
                for j in bank_tiles(b):
                    last = nc.tensor.transpose(
                        z_ps[0:PN, b, (j % TPB) * (C + 1):(j % TPB + 1) * (C + 1)],
                        agg0[:, j * PN:(j + 1) * PN], ident[0:C + 1, 0:C + 1])
                last.then_inc(turned0, 1)

            def batch_sums(layer):
                for n, (of, wait, ready) in enumerate(((h, h_ready, sums_ready), (sq, squared, vars_ready))):
                    for j in range(NT):
                        if j % TPB == 0:
                            pe.wait_ge(wait[layer], j // TPB + 1)
                        last = nc.tensor.matmul(m_ps[0:PN, n, 0:C], ones[0:PN, 0:PN], of[:, j, :],
                                                start=(j == 0), stop=(j == NT - 1))
                    last.then_inc(ready[layer], 1)

            batch_sums(0)

            with pe.Fori(0, NCH // SLOTS) as i:
                for s in range(SLOTS):
                    c = i * SLOTS + s
                    pe.wait_ge(gathered[s], i * (CH * 16) + (NCH // SLOTS + 1) * CH * 16)
                    pe.wait_ge(ea_loaded[s], i * 16 + 16)
                    pe.wait_ge(a_free, c + 1)
                    for t in range(CH):
                        last = nc.tensor.matmul(t_ps[:, s % 2, (t // SUP) * WIN:(t // SUP + 1) * WIN],
                                                rows[:, s, t, :],
                                                hot[:, bass.ds(c * CH + t, 1), :].rearrange("p a w -> p (a w)"),
                                                start=(t % SUP == 0), stop=(t % SUP == SUP - 1))
                    last.then_inc(summed, 1)

            with pe.If(flag > 0):
                with pe.Fori(0, T) as t:
                    with pe.Fori(0, NR) as r:
                        n = (t + T) * NR + r
                        pe.wait_ge(fb_fetched, (t + (T + 1)) * 16)
                        pe.wait_ge(fb_ea, t * 16 + 16)
                        pe.wait_ge(fb_w, n + 1)
                        nc.tensor.matmul(t_ps[:, 0, 0:RW], rows[:, 0, 0, :], fb_hot[:, :],
                                         start=True, stop=True).then_inc(fb_t, 1)

            pe.wait_ge(agg1_done, 2)
            for n, (a, e) in enumerate(HCH):
                if n >= 2:
                    pe.wait_ge(hid_ready, n - 1)
                nc.tensor.matmul(m_ps[:, n % 2, 0:e - a], w1[:, :], agg1[:, a:e],
                                 start=True, stop=True).then_inc(hid_ps_ready, 1)
            for b in range(NB):
                for j in bank_tiles(b):
                    pe.wait_ge(hid_ready, -(-(j + 1) * PN // MMCOL))
                    last = nc.tensor.matmul(z_ps[0:PN, b, (j % TPB) * C:(j % TPB + 1) * C],
                                            hid[:, j * PN:(j + 1) * PN], w2[:, :], start=True, stop=True)
                last.then_inc(h1_ps_ready, 1)
            batch_sums(1)

        @block.scalar
        def _(act):
            def lay_out(c, s):
                nc.scalar.copy(idx[:, s, :], src_col[:, bass.ds(c * CH, CH)]).then_inc(idx_ready, 1)

            act.wait_ge(src_col_ready, 1)
            for c in range(AHEAD):
                nc.scalar.copy(idx[:, c, :], src_col[:, c * CH:(c + 1) * CH]).then_inc(idx_ready, 1)
            for g in range(-(-NT // 4)):
                act.wait_ge(xt_turned, g + 1)
                n = min(4, NT - 4 * g) * PN
                nc.scalar.copy(xt[:, 4 * g * PN:4 * g * PN + n], t_ps[0:C, g % 2, 0:n]).then_inc(xt_ready, 1)
            act.wait_ge(xroot_done, 1)
            for b in range(NB):
                ts = bank_tiles(b)
                last = nc.scalar.copy(xroot[:, ts[0]:ts[-1] + 1, :],
                                      z_ps[0:PN, b, 0:len(ts) * C].rearrange("p (t c) -> p t c", c=C))
            last.then_inc(xroot_ready, 1)

            def copy_z(zs, ready, release=None):
                for half in range(2):
                    last = nc.scalar.copy(
                        z_sb[:, zs, 2 * half:2 * half + 2, :, :],
                        z_ps[:, 2 * zs + half, 0:2 * ZW].rearrange("p (w k n) -> p w k n", w=2, k=KIN))
                    last.then_inc(ready, 1)

            with act.Fori(0, NCH // SLOTS) as i:
                for s in range(SLOTS):
                    c = i * SLOTS + s
                    act.wait_ge(gathered[s], i * (CH * 16) + CH * 16)
                    lay_out(c + AHEAD, s)
                    act.wait_ge(summed, c + (SLOTS + 1))
                    act.wait_ge(t_free, c + 1)
                    nc.scalar.copy(
                        z_sb[:, s % 2, 0:2, :, :],
                        z_ps[:, 2 * (s % 2), 0:2 * ZW].rearrange("p (w k n) -> p w k n", w=2, k=KIN))
                    nc.scalar.copy(
                        z_sb[:, s % 2, 2:4, :, :],
                        z_ps[:, 2 * (s % 2) + 1, 0:2 * ZW].rearrange("p (w k n) -> p w k n", w=2, k=KIN)
                    ).then_inc(zsb_ready, 1)
                    act.wait_ge(zsb_ready, c + 1)
                    act.sem_inc(z_free, 1)

            act.wait_ge(flag_ready, 1)
            flag = act.value_load(missed_any[0:1, 0:1], min_val=0, max_val=1 << 20)
            with act.If(flag > 0):
                with act.Fori(0, T) as t:
                    act.wait_ge(fb_added, t * NR + 1)
                    nc.scalar.copy(fb_idx[:, 0:1], src_col[:, bass.ds(t, 1)]).then_inc(fb_idx_ready, 1)
                    with act.Fori(0, NR) as r:
                        n = t * NR + r
                        act.wait_ge(fb_z, n + 1)
                        nc.scalar.copy(z_sb[:, 0, 0:2, :, :],
                                       z_ps[:, 0, 0:2 * ZW].rearrange("p (w k n) -> p w k n", w=2, k=KIN))
                        nc.scalar.copy(z_sb[:, 0, 2:4, :, :],
                                       z_ps[:, 1, 0:2 * ZW].rearrange("p (w k n) -> p w k n", w=2, k=KIN)
                                       ).then_inc(fb_zsb, 1)

            def batch_and_layer_norm(layer):
                for b in range(NB):
                    ts = bank_tiles(b)
                    act.wait_ge(centred[layer], b + 1)
                    nc.scalar.activation(sq[:, ts[0]:ts[-1] + 1, :], h[:, ts[0]:ts[-1] + 1, :],
                                         ACT.Square).then_inc(squared[layer], 1)
                act.wait_ge(var_ready[layer], 1)
                nc.scalar.activation(std[:, :], var[:, :], ACT.Sqrt).then_inc(std_ready[layer], 1)
                if layer == 0:
                    for b in range(NB):
                        ts = bank_tiles(b)
                        act.wait_ge(y_ready, b + 1)
                        nc.scalar.activation(sq[:, ts[0]:ts[-1] + 1, :], h[:, ts[0]:ts[-1] + 1, :],
                                             ACT.Exp).then_inc(exp_ready, 1)
                for b in range(NB):
                    ts = bank_tiles(b)
                    act.wait_ge(ln_centred[layer], b + 1)
                    nc.scalar.activation(sq[:, ts[0]:ts[-1] + 1, :], h[:, ts[0]:ts[-1] + 1, :],
                                         ACT.Square).then_inc(ln_squared[layer], 1)
                act.wait_ge(ln_var_ready[layer], 1)
                nc.scalar.activation(ln_std[:, :], ln_var[:, :], ACT.Sqrt).then_inc(ln_std_ready[layer], 1)

            batch_and_layer_norm(0)
            for b in range(NB):
                ts = bank_tiles(b)
                act.wait_ge(x1_ready, b + 1)
                act.dma_start(node_major(x1_dram)[:, ts[0]:ts[-1] + 1, :],
                              x1[:, ts[0]:ts[-1] + 1, :]).then_inc(x1_stored, 16)

            with act.Fori(0, NCH // SLOTS) as i:
                for s in range(SLOTS):
                    act.wait_ge(gathered[s], i * (CH * 16) + (NCH // SLOTS + 1) * CH * 16)
                    lay_out(i * SLOTS + (s + AHEAD), s)

            with act.If(flag > 0):
                with act.Fori(0, T) as t:
                    act.wait_ge(fb_added, (t + T) * NR + 1)
                    nc.scalar.copy(fb_idx[:, 0:1], src_col[:, bass.ds(t, 1)]).then_inc(fb_idx_ready, 1)

            for n, (a, e) in enumerate(HCH):
                act.wait_ge(hid_ps_ready, n + 1)
                nc.scalar.activation(hid[:, a:e], m_ps[:, n % 2, 0:e - a], ACT.Relu,
                                     bias=b1[:, 0:1]).then_inc(hid_ready, 1)
            batch_and_layer_norm(1)

        @block.vector
        def _(dve):
            steps = [0]

            def then_wait(instruction):
                steps[0] += 1
                instruction.then_inc(dve_step, 1)
                dve.wait_ge(dve_step, steps[0])

            nc.vector.memset(src_rows[0:TB, BLK - 1, :], 0).then_inc(pads_set, 1)
            nc.vector.memset(dst_rows[0:TB, BLK - 1, :], int(NOWHERE)).then_inc(pads_set, 1)
            nc.vector.memset(ea3_rows[0:TB, BLK - 1, :, :], 0.0).then_inc(pads_set, 1)
            nc.vector.memset(ones[:, :], 1.0).then_inc(ones_ready, 1)
            dve.wait_ge(src_loaded, 48)
            nc.vector.tensor_copy(src_rows_f[:, 0:BLK - 1, :], src_rows[:, 0:BLK - 1, :])
            nc.vector.tensor_copy(src_rows_f[0:TB, BLK - 1, :], src_rows[0:TB, BLK - 1, :]).then_inc(src_f_ready, 1)
            dve.wait_ge(dst_loaded, 48)
            nc.vector.tensor_copy(dst_rows_f[:, 0:BLK - 1, :], dst_rows[:, 0:BLK - 1, :])
            nc.vector.tensor_copy(dst_rows_f[0:TB, BLK - 1, :], dst_rows[0:TB, BLK - 1, :]).then_inc(dst_f_ready, 1)
            dve.wait_ge(src_turned, 1)
            nc.vector.tensor_copy(src_col[:, T:T + AHEAD * CH], m_ps[:, 0, 0:AHEAD * CH])
            nc.vector.tensor_copy(src_col[:, 0:T], m_ps[:, 0, 0:T]).then_inc(src_col_ready, 1)
            dve.wait_ge(dst_turned, 1)
            nc.vector.tensor_copy(base[0:1, :], m_ps[0:1, 1, 0:T:SUP])
            nc.vector.tensor_copy(dst_col[:, :], m_ps[:, 1, 0:T]).then_inc(dst_col_ready, 1)
            nc.vector.memset(rows[:, :, :, C:P], 1.0).then_inc(summed, SLOTS)
            nc.vector.memset(agg0[:, :], 0.0)
            nc.vector.memset(agg1[:, :], 0.0)
            nc.vector.memset(basis[:, :, NK], 1.0)
            nc.vector.memset(basis[:, T:T + CH, 0:NK], 0.0)
            then_wait(nc.vector.memset(rel[:, T:T + CH], -1.0))
            dve.wait_ge(iota_ready, 1)
            nc.vector.tensor_copy(iota_f[:, :], iota_i[:, :])
            dve.wait_ge(base_spread, 1)
            dve.wait_ge(dst_col_ready, 1)
            then_wait(nc.vector.tensor_tensor(
                rel[:, 0:T].rearrange("p (g s) -> p g s", s=SUP),
                dst_col[:, :].rearrange("p (g s) -> p g s", s=SUP),
                m_ps[:, 0, 0:T // SUP].rearrange("p (g s) -> p g s", s=1).to_broadcast([P, T // SUP, SUP]),
                ALU.subtract))
            then_wait(nc.vector.tensor_scalar(real[:, :], dst_col[:, :], 0.0, None, ALU.is_ge))
            nc.vector.scalar_tensor_tensor(out=missed[:, :], in0=rel[:, 0:T], scalar=0.0, in1=real[:, :],
                                           op0=ALU.is_lt, op1=ALU.mult)
            then_wait(nc.vector.scalar_tensor_tensor(out=missed2[:, :], in0=rel[:, 0:T], scalar=float(WIN),
                                                     in1=real[:, :], op0=ALU.is_ge, op1=ALU.mult))
            then_wait(nc.vector.tensor_tensor(missed[:, :], missed[:, :], missed2[:, :], ALU.add))
            nc.vector.reduce_sum(missed_row[:, :], missed[:, :], axis=AX.X).then_inc(missed_ready, 1)
            then_wait(nc.vector.scalar_tensor_tensor(out=missed_dst[:, :], in0=dst_col[:, :], scalar=-NOWHERE,
                                                     in1=missed[:, :], op0=ALU.add, op1=ALU.mult))
            then_wait(nc.vector.tensor_scalar(missed_dst[:, :], missed_dst[:, :], NOWHERE, None, ALU.add))
            dve.wait_ge(missed_summed, 1)
            nc.vector.tensor_copy(missed_any[0:1, 0:1], m_ps[0:1, 1, 0:1]).then_inc(flag_ready, 1)
            for d in range(D):
                dve.wait_ge(ea3_turned, d + 1)
                last = nc.vector.tensor_scalar(w_lohi[:, d, :, 1], z_ps[:, d, 0:T], 0.0, 1.0, ALU.max, ALU.min)
            last.then_inc(basis_in, 1)
            dve.wait_ge(basis_in, 1)
            then_wait(nc.vector.tensor_scalar(w_lohi[:, :, :, 0], w_lohi[:, :, :, 1], -1.0, 1.0, ALU.mult, ALU.add))
            for hi in range(2):
                last = nc.vector.tensor_tensor(w_pair[:, :, 2 * hi:2 * hi + 2], w_lohi[:, 0, :, :],
                                               w_lohi[:, 1, :, hi:hi + 1].to_broadcast([P, T, 2]), ALU.mult)
            then_wait(last)
            for hi in range(2):
                last = nc.vector.tensor_tensor(basis[:, 0:T, 4 * hi:4 * hi + 4], w_pair[:, :, :],
                                               w_lohi[:, 2, :, hi:hi + 1].to_broadcast([P, T, 4]), ALU.mult)
            then_wait(last)

            def build(c, half, n, with_wait=True):
                nc.vector.tensor_tensor(
                    hot[:, bass.ds(c * CH, CH), :],
                    iota_f[:, 0:WIN].rearrange("p (a w) -> p a w", a=1).to_broadcast([P, CH, WIN]),
                    rel[:, bass.ds(c * CH, CH)].rearrange("p (t a) -> p t a", a=1).to_broadcast([P, CH, WIN]),
                    ALU.is_equal).then_inc(hot_ready, 1)
                dve.wait_ge(hot_ready, n)
                if with_wait:
                    dve.wait_ge(summed, n - 2 + SLOTS)
                nc.vector.tensor_tensor(
                    whot[:, half, :, :].rearrange("p t (k w) -> p t k w", k=KIN),
                    hot[:, bass.ds(c * CH, CH), :].rearrange("p t (a w) -> p t a w", a=1
                                                             ).to_broadcast([P, CH, KIN, WIN]),
                    basis[:, bass.ds(c * CH, CH), :].rearrange("p t (k a) -> p t k a", a=1
                                                               ).to_broadcast([P, CH, KIN, WIN]),
                    ALU.mult).then_inc(whot_ready, 1)

            nc.vector.memset(fb_rel[:, :], 0.0).then_inc(z_free, 2)
            nc.vector.memset(fb_hot[:, :], 0.0).then_inc(t_free, 2)
            nc.vector.memset(fb_whot[:, :, :, :], 0.0).then_inc(fb_added, 1)

            def add_windows(c, bank, into, parts, ready, count, free, added):
                at = [dve.value_load(base[0:1, bass.ds(c * WPC + w, 1)], min_val=0, max_val=N - 1)
                      for w in range(WPC)]
                dve.wait_ge(ready, count)
                for w in range(WPC):
                    view = into[:, bass.ds(at[w], WIN)]
                    nc.vector.tensor_tensor(view, view, t_ps[0:parts, bank, w * WIN:(w + 1) * WIN],
                                            ALU.add).then_inc(added, 1)
                    dve.wait_ge(added, c * WPC + (w + 1))
                dve.sem_inc(free, 1)

            build(0, 0, 1, False)
            with dve.Fori(0, NCH // SLOTS) as i:
                for s in range(SLOTS):
                    c = i * SLOTS + s
                    build(c + 1, (s + 1) % 2, c + 2)
                    add_windows(c, s % 2, agg0, C + 1, t_ready, c + 1, t_free, added0)
            nc.vector.memset(fb_rel[:, :], 0.0).then_inc(agg0_done, 1)

            def missed_ranges(t, tiles_before, weighted, into, parts):
                k0 = (t + tiles_before) * NR
                nc.vector.tensor_copy(fb_rel[:, 0:1], missed_dst[:, bass.ds(t, 1)]).then_inc(fb_step, 1)
                with dve.Fori(0, NR) as r:
                    n = k0 + r
                    dve.wait_ge(fb_step, n + t + (tiles_before + 1))
                    one_hot = nc.vector.tensor_scalar(fb_hot[:, :], iota_f[:, :], fb_rel[:, 0:1], None, ALU.is_equal)
                    one_hot.then_inc(fb_step, 1)
                    dve.wait_ge(fb_step, n + t + (tiles_before + 2))
                    if weighted:
                        for w in range(WPC):
                            last = nc.vector.tensor_tensor(
                                fb_whot[:, w, :, :],
                                fb_hot[:, w * WIN:(w + 1) * WIN].rearrange("p (a n) -> p a n", a=1
                                                                           ).to_broadcast([P, KIN, WIN]),
                                basis[:, bass.ds(t, 1), :].rearrange("p a k -> p k a").to_broadcast([P, KIN, WIN]),
                                ALU.mult)
                        last.then_inc(fb_w, 1)
                    else:
                        dve.sem_inc(fb_w, 1)
                    nc.vector.tensor_scalar(fb_rel[:, 0:1], fb_rel[:, 0:1], float(-RW), None, ALU.add)
                    dve.wait_ge(fb_t, n + 1)
                    view = into[:, bass.ds(r * RW, RW)]
                    nc.vector.tensor_tensor(view, view, t_ps[0:parts, 0, 0:RW], ALU.add).then_inc(fb_added, 1)
                    dve.wait_ge(fb_added, n + 2)

            dve.wait_ge(flag_ready, 1)
            flag = dve.value_load(missed_any[0:1, 0:1], min_val=0, max_val=1 << 20)
            with dve.If(flag > 0):
                dve.wait_ge(agg0_done, 1)
                with dve.Fori(0, T) as t:
                    missed_ranges(t, 0, True, agg0, C + 1)
            dve.wait_ge(agg0_done, 1)
            nc.vector.memset(fb_rel[:, :], 0.0).then_inc(agg0_done, 1)

            def tiles_of(a, b):
                ts = bank_tiles(b)
                return a[:, ts[0]:ts[-1] + 1, :]

            def spread(v, b):
                return v.rearrange("p (a c) -> p a c", a=1).to_broadcast([PN, len(bank_tiles(b)), C])

            def per_node(v, b):
                ts = bank_tiles(b)
                return v[:, ts[0]:ts[-1] + 1].rearrange("p (t a) -> p t a", a=1).to_broadcast([PN, len(ts), C])

            def batch_norm(layer, gamma, beta):
                dve.wait_ge(sums_ready[layer], 1)
                then_wait(nc.vector.tensor_scalar(mean[:, :], m_ps[0:PN, 0, 0:C], 1.0 / N, None, ALU.mult))
                for b in range(NB):
                    nc.vector.tensor_tensor(tiles_of(h, b), tiles_of(h, b), spread(mean[:, :], b),
                                            ALU.subtract).then_inc(centred[layer], 1)
                dve.wait_ge(vars_ready[layer], 1)
                nc.vector.tensor_scalar(var[:, :], m_ps[0:PN, 1, 0:C], 1.0 / N, EPS, ALU.mult, ALU.add
                                        ).then_inc(var_ready[layer], 1)
                dve.wait_ge(std_ready[layer], 1)
                then_wait(nc.vector.reciprocal(std[:, :], std[:, :]))
                then_wait(nc.vector.tensor_tensor(scale[:, :], std[:, :], gamma, ALU.mult))
                for b in range(NB):
                    last = nc.vector.tensor_tensor(tiles_of(h, b), tiles_of(h, b), spread(scale[:, :], b), ALU.mult)
                then_wait(last)
                for b in range(NB):
                    last = nc.vector.tensor_tensor(tiles_of(h, b), tiles_of(h, b), spread(beta, b), ALU.add)
                    if layer == 0:
                        last.then_inc(y_ready, 1)
                if layer == 0:
                    dve.wait_ge(y_ready, NB)
                else:
                    then_wait(last)

            def layer_norm(layer, to, ready):
                for b in range(NB):
                    ts = bank_tiles(b)
                    last = nc.vector.tensor_reduce(ln_sum[:, ts[0]:ts[-1] + 1], tiles_of(h, b), AX.X, ALU.add)
                then_wait(last)
                then_wait(nc.vector.tensor_scalar(ln_mean[:, :], ln_sum[:, :], 1.0 / C, None, ALU.mult))
                for b in range(NB):
                    nc.vector.tensor_tensor(tiles_of(h, b), tiles_of(h, b), per_node(ln_mean, b),
                                            ALU.subtract).then_inc(ln_centred[layer], 1)
                for b in range(NB):
                    ts = bank_tiles(b)
                    dve.wait_ge(ln_squared[layer], b + 1)
                    last = nc.vector.tensor_reduce(ln_sum[:, ts[0]:ts[-1] + 1], tiles_of(sq, b), AX.X, ALU.add)
                then_wait(last)
                nc.vector.tensor_scalar(ln_var[:, :], ln_sum[:, :], 1.0 / C, EPS, ALU.mult, ALU.add
                                        ).then_inc(ln_var_ready[layer], 1)
                dve.wait_ge(ln_std_ready[layer], 1)
                then_wait(nc.vector.reciprocal(ln_rstd[:, :], ln_std[:, :]))
                dve.wait_ge(ln_centred[layer], NB)
                for b in range(NB):
                    nc.vector.tensor_tensor(tiles_of(to, b), tiles_of(h, b), per_node(ln_rstd, b),
                                            ALU.mult).then_inc(ready, 1)

            dve.wait_ge(xroot_ready, 1)
            for b in range(NB):
                ts = bank_tiles(b)
                n = len(ts)
                dve.wait_ge(turned0, b + 1)
                turned = z_ps[0:PN, b, 0:n * (C + 1)].rearrange("p (t c) -> p t c", c=C + 1)
                inv = inv_cnt[:, ts[0]:ts[-1] + 1]
                then_wait(nc.vector.tensor_scalar(inv, turned[:, :, C], 1.0, None, ALU.max))
                then_wait(nc.vector.reciprocal(inv, inv))
                then_wait(nc.vector.tensor_tensor(tiles_of(h, b), turned[:, :, 0:C], per_node(inv_cnt, b), ALU.mult))
                nc.vector.tensor_tensor(tiles_of(h, b), tiles_of(h, b), tiles_of(xroot, b), ALU.add
                                        ).then_inc(h_ready[0], 1)
            dve.wait_ge(vecs_loaded, 80)
            batch_norm(0, vecs[:, 0, :], vecs[:, 1, :])
            for b in range(NB):
                last = nc.vector.scalar_tensor_tensor(out=tiles_of(x1, b), in0=tiles_of(h, b), scalar=0.0,
                                                      in1=tiles_of(x_nm, b), op0=ALU.max, op1=ALU.add)
            then_wait(last)
            for b in range(NB):
                dve.wait_ge(exp_ready, b + 1)
                last = nc.vector.scalar_tensor_tensor(out=tiles_of(h, b), in0=tiles_of(sq, b), scalar=1.0,
                                                      in1=tiles_of(x1, b), op0=ALU.min, op1=ALU.add)
            then_wait(last)
            layer_norm(0, x1, x1_ready)

            nc.vector.memset(fb_rel[:, :], 0.0).then_inc(a_free, 2)
            with dve.Fori(0, NCH // SLOTS) as i:
                for s in range(SLOTS):
                    c = i * SLOTS + s
                    add_windows(c, s % 2, agg1, P, summed, c + (NCH + SLOTS + 1), a_free, added1)
            nc.vector.memset(fb_rel[:, :], 0.0).then_inc(agg1_done, 1)
            with dve.If(flag > 0):
                dve.wait_ge(agg1_done, 1)
                with dve.Fori(0, T) as t:
                    missed_ranges(t, T, False, agg1, P)
            dve.wait_ge(agg1_done, 1)
            nc.vector.memset(fb_rel[:, :], 0.0).then_inc(agg1_done, 1)

            for b in range(NB):
                ts = bank_tiles(b)
                dve.wait_ge(h1_ps_ready, b + 1)
                nc.vector.tensor_tensor(tiles_of(h, b),
                                        z_ps[0:PN, b, 0:len(ts) * C].rearrange("p (t c) -> p t c", c=C),
                                        spread(vecs[:, 2, :], b), ALU.add).then_inc(h_ready[1], 1)
            batch_norm(1, vecs[:, 3, :], vecs[:, 4, :])
            for b in range(NB):
                last = nc.vector.tensor_tensor(tiles_of(h, b), tiles_of(h, b), tiles_of(x1, b), ALU.add)
            then_wait(last)
            layer_norm(1, res, out_ready)


_INS = ["x", "src", "dst", "edge_attr_3", "edge_attr_64", "L0_gnn_W", "L0_gnn_root", "L0_gnn_gamma",
        "L0_gnn_beta", "L1_gnn_W1", "L1_gnn_b1", "L1_gnn_W2", "L1_gnn_b2", "L1_gnn_bn_gamma", "L1_gnn_bn_beta"]


def kernel(**inputs):
    import numpy as np
    from concourse import bacc
    from concourse.bass_utils import run_bass_kernel_spmd

    nc = bacc.Bacc("TRN2", target_bir_lowering=False, num_devices=1)
    arrays, args = {}, []
    for name in _INS:
        a = np.ascontiguousarray(inputs[name])
        arrays[f"in_{name}"] = a
        args.append(nc.dram_tensor(f"in_{name}", a.shape, mybir.dt.from_np(a.dtype), kind="ExternalInput").ap())
    out = nc.dram_tensor("out", inputs["x"].shape, F32, kind="ExternalOutput").ap()
    gnn_two_layers(nc, *args, out)
    got = run_bass_kernel_spmd(nc, [arrays], core_ids=[0])
    return got.results[0]["out"]
```

```python
from contextlib import ExitStack

import concourse.bass as bass
from concourse import mybir

F32 = mybir.dt.float32
I32 = mybir.dt.int32
BF16 = mybir.dt.bfloat16
ALU = mybir.AluOpType
ACT = mybir.ActivationFunctionType
AX = mybir.AxisListType


def gnn_two_layers(nc, x, src, dst, ea3, ea64, wk_d, root_d, gamma0, beta0,
                   w1_d, b1_d, w2_d, b2_d, gamma1, beta1, out):
    P = 128
    N, C = x.shape
    E = src.shape[0]
    NK = wk_d.shape[0]
    HID = w1_d.shape[1]
    D = ea3.shape[1]
    SLOTS = 4
    CH = 8
    T = -(-E // (P * CH * SLOTS)) * CH * SLOTS
    NCH = T // CH
    AHEAD = SLOTS
    SUP = 2
    WPC = CH // SUP
    GATHERED0 = CH * 16
    GATHERED1 = (CH - 1) * 16
    PICK = NCH + 2
    SPLIT = 3
    WIN = 24
    KIN = NK + 1
    ZW = KIN * WIN
    RW = WPC * WIN
    NR = -(-(N + WIN) // RW)
    NPAD = NR * RW
    PN = 125
    NT = N // PN
    TPB = 7
    NB = -(-NT // TPB)
    FULL = E // P
    REST = E - FULL * P
    BLK = -(-T // P)
    LASTROWS = FULL - (BLK - 1) * P
    TB = T - (BLK - 1) * P
    NOWHERE = -8192.0
    EPS = 1e-5
    assert N == PN * NT and NB <= 4 and BLK == 4 and D == 3 and NK == 8
    assert 0 <= LASTROWS < TB and P == 2 * C and HID == P and FULL == T - 1

    ctx = ExitStack()
    with ctx:
        def sb(name, shape, dt=F32):
            return ctx.enter_context(nc.sbuf_tensor(name, shape, dt))

        def sem(name):
            return ctx.enter_context(nc.semaphore(name))

        src_rows = sb("src_rows", [P, BLK, P], I32)
        dst_rows = sb("dst_rows", [P, BLK, P], I32)
        src_col = sb("src_col", [P, T + AHEAD * CH], I32)
        idx = sb("idx", [P, SLOTS, CH], I32)
        dst_col = sb("dst_col", [P, T])
        rel = sb("rel", [P, T + CH])
        missed_dst = sb("missed_dst", [P, T])
        missed_row = sb("missed_row", [P, 1])
        missed_any = sb("missed_any", [1, 1], I32)
        base = sb("base", [1, T // SUP], I32)
        basis = sb("basis", [P, T + CH, KIN])
        hot = sb("hot", [P, T + CH, WIN])
        place = hot[:, :, :].rearrange("p t w -> p (t w)")
        sizes = [BLK * P * D, BLK * P, BLK * P, D * T * 2, T * 4, T, T, T]
        ends = [sum(sizes[:n + 1]) for n in range(len(sizes))]
        ea3_rows, src_rows_f, dst_rows_f, w_lohi, w_pair, real, missed, missed2 = (place[:, e - n:e] for n, e in zip(sizes, ends))
        assert ends[-1] <= (T + CH) * WIN and N <= (T + CH) * WIN
        ea3_rows = ea3_rows.rearrange("p (b e d) -> p b e d", b=BLK, e=P)
        src_rows_f = src_rows_f.rearrange("p (b e) -> p b e", b=BLK)
        dst_rows_f = dst_rows_f.rearrange("p (b e) -> p b e", b=BLK)
        w_lohi = w_lohi.rearrange("p (d t s) -> p d t s", d=D, s=2)
        w_pair = w_pair.rearrange("p (t s) -> p t s", s=4)
        hid = place[:, 0:N]
        whot = sb("whot", [P, 2, CH, ZW])
        rows = sb("rows", [P, SLOTS, CH, P])
        z_sb = sb("z_sb", [P, 2, WPC, KIN, WIN])
        agg0 = sb("agg0", [C + 1, NPAD])
        agg1 = sb("agg1", [P, NPAD])
        x_nm = sb("x_nm", [PN, NT, C])
        xt = sb("xt", [C, N])
        xroot = sb("xroot", [PN, NT, C])
        ident = sb("ident", [P, P])
        ones = sb("ones", [P, P])
        iota_i = sb("iota_i", [P, RW], I32)
        iota_f = sb("iota_f", [P, RW])
        wk = sb("wk", [C, NK, C])
        root = sb("root", [C, C])
        w1 = sb("w1", [P, HID])
        w2 = sb("w2", [HID, C])
        b1 = sb("b1", [HID, 1])
        vecs = sb("vecs", [PN, 5, C])
        h = sb("h", [PN, NT, C])
        sq = sb("sq", [PN, NT, C])
        x1 = sb("x1", [PN, NT, C])
        res = xroot
        bank_sums = sb("bank_sums", [PN, 2, NB, C])
        inv_cnt = sb("inv_cnt", [PN, NT])
        mean = sb("mean", [PN, C])
        var = sb("var", [PN, C])
        std = sb("std", [PN, C])
        scale = sb("scale", [PN, C])
        ln_sum = sb("ln_sum", [PN, NT])
        ln_mean = sb("ln_mean", [PN, NT])
        ln_var = sb("ln_var", [PN, NT])
        ln_std = sb("ln_std", [PN, NT])
        ln_rstd = sb("ln_rstd", [PN, NT])
        fb_idx = sb("fb_idx", [P, 1], I32)
        fb_rel = sb("fb_rel", [P, 2])
        fb_hot = sb("fb_hot", [P, RW])
        fb_whot = sb("fb_whot", [P, WPC, KIN, WIN])
        src_wide = sb("src_wide", [PN, 2, P], I32)
        node_i = sb("node_i", [PN, NT], I32)
        node_f = sb("node_f", [PN, NT])
        pick_hot = sb("pick_hot", [PN, 2, NT, P], BF16)
        table = sb("table", [PN, NT, SPLIT, C], BF16)
        x1_dram = nc.dram_tensor("x1_scratch", (N, C), F32).ap()

        z_ps = ctx.enter_context(nc.psum_tensor("z_ps", [P, 4, 512], F32))
        t_ps = ctx.enter_context(nc.psum_tensor("t_ps", [P, 2, 512], F32))
        m_ps = ctx.enter_context(nc.psum_tensor("m_ps", [P, 2, 512], F32))

        pads_set = sem("pads_set")
        src_loaded, dst_loaded, ea3_loaded = sem("src_loaded"), sem("dst_loaded"), sem("ea3_loaded")
        x_loaded, weights_loaded, vecs_loaded = sem("x_loaded"), sem("weights_loaded"), sem("vecs_loaded")
        pool_step = sem("pool_step")
        aggs_zeroed = sem("aggs_zeroed")
        ident_ready, iota_ready, ones_ready = sem("ident_ready"), sem("iota_ready"), sem("ones_ready")
        src_f_ready, dst_f_ready = sem("src_f_ready"), sem("dst_f_ready")
        src_turned, dst_turned, ea3_turned = sem("src_turned"), sem("dst_turned"), sem("ea3_turned")
        src_col_ready, dst_col_ready, basis_in = sem("src_col_ready"), sem("dst_col_ready"), sem("basis_in")
        base_spread, missed_ready, missed_summed, flag_ready = (
            sem("base_spread"), sem("missed_ready"), sem("missed_summed"), sem("flag_ready"))
        xt_turned, xt_ready, xroot_done, xroot_ready = (
            sem("xt_turned"), sem("xt_ready"), sem("xroot_done"), sem("xroot_ready"))
        idx_ready = sem("idx_ready")
        begun = sem("begun")
        gathered = [sem(f"gathered{s}") for s in range(SLOTS)]
        summed = sem("summed")
        hot_ready, whot_ready = sem("hot_ready"), sem("whot_ready")
        z_free, zsb_ready = sem("z_free"), sem("zsb_ready")
        t_ready, t_free = sem("t_ready"), sem("t_free")
        added0, added1 = sem("added0"), sem("added1")
        agg0_done, agg1_done = sem("agg0_done"), sem("agg1_done")
        ea_rest_loaded = sem("ea_rest_loaded")
        ea_loaded = [sem(f"ea_loaded{s}") for s in range(SLOTS)]
        a_free = sem("a_free")
        fb_fetched, fb_idx_ready, fb_ea = sem("fb_fetched"), sem("fb_idx_ready"), sem("fb_ea")
        fb_w, fb_z, fb_zsb, fb_t, fb_step = sem("fb_w"), sem("fb_z"), sem("fb_zsb"), sem("fb_t"), sem("fb_step")
        fb_added = sem("fb_added")
        turned0 = sem("turned0")
        h_ready = [sem("h0_ready"), sem("h1_ready")]
        h_summed = [sem("h0_summed"), sem("h1_summed")]
        sq_summed = [sem("sq0_summed"), sem("sq1_summed")]
        sums_ready = [sem("sums0_ready"), sem("sums1_ready")]
        centred = [sem("centred0"), sem("centred1")]
        squared = [sem("squared0"), sem("squared1")]
        vars_ready = [sem("vars0_ready"), sem("vars1_ready")]
        var_ready = [sem("var0_ready"), sem("var1_ready")]
        std_ready = [sem("std0_ready"), sem("std1_ready")]
        y_ready, exp_ready = sem("y_ready"), sem("exp_ready")
        ln_centred = [sem("ln_centred0"), sem("ln_centred1")]
        ln_squared = [sem("ln_squared0"), sem("ln_squared1")]
        ln_var_ready = [sem("ln_var0_ready"), sem("ln_var1_ready")]
        ln_std_ready = [sem("ln_std0_ready"), sem("ln_std1_ready")]
        x1_ready, x1_stored, out_ready, out_stored = (
            sem("x1_ready"), sem("x1_stored"), sem("out_ready"), sem("out_stored"))
        hid_ps_ready, hid_ready, h1_ps_ready = sem("hid_ps_ready"), sem("hid_ready"), sem("h1_ps_ready")
        dve_step = sem("dve_step")
        node_ready = sem("node_ready")
        part_added = sem("part_added")
        src_wide_loaded = [sem("src_wide0_loaded"), sem("src_wide1_loaded")]
        pick_hot_ready, src_wide_free = sem("pick_hot_ready"), sem("src_wide_free")
        table_ready, picked, pick_summed = sem("table_ready"), sem("picked"), sem("pick_summed")

        block = ctx.enter_context(nc.Block())

        def node_major(a):
            return a.rearrange("(t p) c -> p t c", p=PN)

        def bank_tiles(b):
            return range(b * TPB, min((b + 1) * TPB, NT))

        ea64_full = ea64[0:FULL * P, :].rearrange("(t p) c -> p t c", p=P)
        MMCOL = 450
        HCH = [(a, min(a + MMCOL, N)) for a in range(0, N, MMCOL)]

        @block.sync
        def _(sp):
            sp.wait_ge(pads_set, 3)

            def load_rows(tile, d, loaded, per):
                lead = (BLK - 1) * P * P
                view = d if per == 1 else d.rearrange("e d -> (e d)")
                sp.dma_start(tile[:, 0:BLK - 1], view[0:lead * per].rearrange(
                    "(b r k) -> r b k", b=BLK - 1, r=P)).then_inc(loaded, 16)
                sp.dma_start(tile[0:LASTROWS, BLK - 1], view[lead * per:FULL * P * per].rearrange(
                    "(r k) -> r k", r=LASTROWS)).then_inc(loaded, 16)
                sp.dma_start(tile[LASTROWS:LASTROWS + 1, BLK - 1, 0:REST * per],
                             view[FULL * P * per:E * per].rearrange("(r k) -> r k", r=1)).then_inc(loaded, 16)

            load_rows(src_rows, src, src_loaded, 1)
            load_rows(dst_rows, dst, dst_loaded, 1)
            load_rows(ea3_rows[:, :, :, :].rearrange("p b e d -> p b (e d)"), ea3, ea3_loaded, D)
            sp.dma_start(x_nm[:, :, :], node_major(x)).then_inc(x_loaded, 16)
            sp.dma_start(root[:, :], root_d).then_inc(weights_loaded, 16)
            sp.dma_start(wk[:, :, :], wk_d.rearrange("k i o -> i k o")).then_inc(weights_loaded, 16)
            sp.dma_start(w1[0:C, :], w1_d).then_inc(weights_loaded, 16)
            sp.dma_start(w1[C:P, :], w1_d).then_inc(weights_loaded, 16)
            sp.dma_start(w2[:, :], w2_d).then_inc(weights_loaded, 16)
            sp.dma_start(b1[:, :], b1_d.rearrange("(p a) -> p a", a=1)).then_inc(weights_loaded, 16)
            for n, v in enumerate((gamma0, beta0, b2_d, gamma1, beta1)):
                sp.dma_start(vecs[:, n, :], v.rearrange("(a c) -> a c", a=1).to_broadcast([PN, C])
                             ).then_inc(vecs_loaded, 16)

            def load_src_wide(c, half):
                sp.wait_ge(src_wide_free, c + 1)
                sp.dma_start(src_wide[:, half, :],
                             src[bass.ds(c * (CH * P), P)].rearrange("(a e) -> a e", a=1).to_broadcast([PN, P])
                             ).then_inc(src_wide_loaded[half], 16)

            def load_src_wide_behind():
                for half in range(2):
                    sp.wait_ge(src_wide_free, NCH + half + 1)
                    sp.dma_start(src_wide[:, half, :],
                                 src[0:P].rearrange("(a e) -> a e", a=1).to_broadcast([PN, P])
                                 ).then_inc(src_wide_loaded[half], 16)

            def load_ea(c, s):
                sp.wait_ge(summed, c + (NCH + 1))
                sp.dma_start(rows[:, s, :, C:P], ea64_full[:, bass.ds(c * CH, CH), :]).then_inc(ea_loaded[s], 16)

            sp.wait_ge(agg0_done, 2)
            with sp.Fori(0, NCH // SLOTS - 1) as i:
                for s in range(SLOTS):
                    load_src_wide(i * SLOTS + s, s % 2)
                    load_ea(i * SLOTS + s, s)
            for s in range(SLOTS - 1):
                load_src_wide(NCH - SLOTS + s, s % 2)
                load_ea(NCH - SLOTS + s, s)
            load_src_wide(NCH - 1, (SLOTS - 1) % 2)
            sp.wait_ge(summed, NCH + NCH)
            sp.dma_start(rows[0:REST, SLOTS - 1, CH - 1, C:P], ea64[FULL * P:E, :]).then_inc(ea_rest_loaded, 16)
            sp.wait_ge(ea_rest_loaded, 16)
            sp.dma_start(rows[:, SLOTS - 1, 0:CH - 1, C:P], ea64_full[:, FULL - CH + 1:FULL, :]).then_inc(
                ea_loaded[SLOTS - 1], 16)

            load_src_wide_behind()
            sp.wait_ge(flag_ready, 1)
            flag = sp.value_load(missed_any[0:1, 0:1], min_val=0, max_val=1 << 20)
            with sp.If(flag > 0):
                sp.wait_ge(agg1_done, 1)
                with sp.Fori(0, FULL) as t:
                    sp.wait_ge(fb_added, (T + t) * NR + 1)
                    sp.dma_start(rows[:, 0, 0, C:P], ea64[bass.ds(t * P, P), :]).then_inc(fb_ea, 16)
                sp.wait_ge(fb_added, (T + FULL) * NR + 1)
                sp.dma_start(rows[0:REST, 0, 0, C:P], ea64[FULL * P:E, :]).then_inc(fb_ea, 16)

            for b in range(NB):
                ts = bank_tiles(b)
                sp.wait_ge(out_ready, b + 1)
                sp.dma_start(node_major(out)[:, ts[0]:ts[-1] + 1, :],
                             res[:, ts[0]:ts[-1] + 1, :]).then_inc(out_stored, 16)
            sp.wait_ge(out_stored, 16 * NB)

        @block.gpsimd
        def _(pool):
            nc.gpsimd.memset(ident[:, :], 0.0).then_inc(pool_step, 1)
            nc.gpsimd.iota(node_i[:, :], pattern=[[PN, NT]], base=0, channel_multiplier=1).then_inc(node_ready, 1)
            nc.gpsimd.iota(iota_i[:, :], pattern=[[1, RW]], base=0, channel_multiplier=0).then_inc(iota_ready, 1)
            pool.wait_ge(pool_step, 1)
            nc.gpsimd.affine_select(out=ident[:, :], in_=ident[:, :], compare_op=ALU.not_equal, fill=1.0,
                                    base=0, pattern=[[-1, P]], channel_multiplier=1).then_inc(ident_ready, 1)
            nc.gpsimd.memset(agg0[:, :], 0.0).then_inc(aggs_zeroed, 1)
            nc.gpsimd.memset(agg1[:, :], 0.0).then_inc(aggs_zeroed, 1)

            def gather(table, chunks_before, first_tile):
                with pool.Fori(0, NCH // SLOTS) as i:
                    for s in range(SLOTS):
                        c = i * SLOTS + (s + chunks_before + 1)
                        pool.wait_ge(idx_ready, c)
                        pool.wait_ge(summed, c)
                        pool.sem_inc(begun, 1)
                        for t in range(first_tile, CH):
                            pool.indirect_dma_start(
                                rows[:, s, t, 0:C], None, table,
                                bass.IndirectOffsetOnAxis(ap=idx[:, s, t:t + 1], axis=0)).then_inc(gathered[s], 16)

            def gather_missed(table, flag, done, tiles_before):
                with pool.If(flag > 0):
                    pool.wait_ge(done, 1)
                    with pool.Fori(0, T) as t:
                        pool.wait_ge(fb_idx_ready, t + (tiles_before + 1))
                        pool.wait_ge(fb_added, (t + tiles_before) * NR + 1)
                        pool.sem_inc(begun, 1)
                        pool.indirect_dma_start(
                            rows[:, 0, 0, 0:C], None, table,
                            bass.IndirectOffsetOnAxis(ap=fb_idx[:, 0:1], axis=0)).then_inc(fb_fetched, 16)

            gather(x, 0, 0)
            pool.wait_ge(flag_ready, 1)
            flag = pool.value_load(missed_any[0:1, 0:1], min_val=0, max_val=1 << 20)
            gather_missed(x, flag, agg0_done, 0)
            pool.wait_ge(x1_stored, 16 * NB)
            gather(x1_dram, NCH, 1)
            gather_missed(x1_dram, flag, agg1_done, T)

        @block.tensor
        def _(pe):
            pe.wait_ge(ident_ready, 1)

            def turn_rows(dstp, rows_of, turned):
                for b in range(BLK):
                    n = P if b < BLK - 1 else TB
                    last = nc.tensor.transpose(dstp[:, b * P:b * P + n], rows_of(b)[0:n, :], ident[0:n, 0:n])
                last.then_inc(turned, 1)

            pe.wait_ge(src_f_ready, 1)
            turn_rows(m_ps[:, 0, :], lambda b: src_rows_f[:, b, :], src_turned)
            pe.wait_ge(dst_f_ready, 1)
            turn_rows(m_ps[:, 1, :], lambda b: dst_rows_f[:, b, :], dst_turned)
            pe.wait_ge(ones_ready, 1)
            pe.wait_ge(src_col_ready, 1)
            pe.wait_ge(dst_col_ready, 1)
            nc.tensor.matmul(m_ps[:, 0, 0:T // SUP], ones[0:1, :], dst_col[0:1, 0:T:SUP],
                             start=True, stop=True).then_inc(base_spread, 1)
            pe.wait_ge(ea3_loaded, 48)
            for d in range(D):
                turn_rows(z_ps[:, d, :], lambda b: ea3_rows[:, b, :, d], ea3_turned)
            pe.wait_ge(missed_ready, 1)
            nc.tensor.matmul(m_ps[0:1, 1, 0:1], missed_row[:, 0:1], ones[:, 0:1],
                             start=True, stop=True).then_inc(missed_summed, 1)
            pe.wait_ge(x_loaded, 16)
            for g in range(-(-NT // 4)):
                if g >= 2:
                    pe.wait_ge(xt_ready, g - 1)
                for j in range(4 * g, min(4 * g + 4, NT)):
                    last = nc.tensor.transpose(t_ps[0:C, g % 2, (j % 4) * PN:(j % 4 + 1) * PN],
                                               x_nm[:, j, :], ident[0:PN, 0:PN])
                last.then_inc(xt_turned, 1)
            pe.wait_ge(xt_ready, -(-NT // 4))
            pe.wait_ge(basis_in, 1)
            pe.wait_ge(weights_loaded, 96)
            for b in range(NB):
                for j in bank_tiles(b):
                    last = nc.tensor.matmul(z_ps[0:PN, b, (j % TPB) * C:(j % TPB + 1) * C],
                                            xt[:, j * PN:(j + 1) * PN], root[:, :], start=True, stop=True)
            last.then_inc(xroot_done, 1)
            pe.wait_ge(xroot_ready, 1)

            def z_out(zs, w):
                return z_ps[:, 2 * zs + w // 2, (w % 2) * ZW:(w % 2 + 1) * ZW]

            def through_kernels(zs, ts, ready):
                for k in range(NK):
                    nc.tensor.matmul(t_ps[0:C, ts, 0:RW], wk[:, k, :], z_sb[0:C, zs, :, k, :],
                                     start=(k == 0), stop=(k == NK - 1))
                nc.tensor.matmul(t_ps[C:C + 1, ts, 0:RW], ones[C:C + 1, 0:1], z_sb[C:C + 1, zs, :, NK, :],
                                 start=True, stop=True).then_inc(ready, 1)

            def pick(n, half):
                pe.wait_ge(pick_hot_ready, n + 1)
                pe.wait_ge(pick_summed, n + 1)
                for j in range(NT):
                    last = nc.tensor.matmul(m_ps[:, half, 0:SPLIT * C], pick_hot[:, half, j, :],
                                            table[:, j, :, :], start=(j == 0), stop=(j == NT - 1))
                last.then_inc(picked, 1)

            with pe.Fori(0, NCH // SLOTS) as i:
                for s in range(SLOTS):
                    c = i * SLOTS + s
                    zs = s % 2
                    pe.wait_ge(gathered[s], i * GATHERED0 + GATHERED0)
                    pe.wait_ge(whot_ready, c + 1)
                    pe.wait_ge(z_free, c + 1)
                    for t in range(CH):
                        last = nc.tensor.matmul(z_out(zs, t // SUP), rows[:, s, t, :], whot[:, zs, t, :],
                                                start=(t % SUP == 0), stop=(t % SUP == SUP - 1))
                    last.then_inc(summed, 1)
                    pe.wait_ge(weights_loaded, 96)
                    pe.wait_ge(zsb_ready, c + 1)
                    pe.wait_ge(t_free, c + 1)
                    through_kernels(zs, zs, t_ready)

            pe.wait_ge(flag_ready, 1)
            flag = pe.value_load(missed_any[0:1, 0:1], min_val=0, max_val=1 << 20)
            with pe.If(flag > 0):
                with pe.Fori(0, T) as t:
                    with pe.Fori(0, NR) as r:
                        n = t * NR + r
                        pe.wait_ge(fb_fetched, t * 16 + 16)
                        pe.wait_ge(fb_w, n + 1)
                        for w in range(WPC):
                            last = nc.tensor.matmul(z_out(0, w), rows[:, 0, 0, :],
                                                    fb_whot[:, w, :, :], start=True, stop=True)
                        last.then_inc(fb_z, 1)
                        pe.wait_ge(weights_loaded, 96)
                        pe.wait_ge(fb_zsb, n + 1)
                        through_kernels(0, 0, fb_t)

            pe.wait_ge(agg0_done, 2)
            for b in range(NB):
                for j in bank_tiles(b):
                    last = nc.tensor.transpose(
                        z_ps[0:PN, b, (j % TPB) * (C + 1):(j % TPB + 1) * (C + 1)],
                        agg0[:, j * PN:(j + 1) * PN], ident[0:C + 1, 0:C + 1])
                last.then_inc(turned0, 1)

            def batch_sums(layer):
                for n, (wait, ready) in enumerate(((h_summed, sums_ready), (sq_summed, vars_ready))):
                    for b in range(NB):
                        pe.wait_ge(wait[layer], b + 1)
                        last = nc.tensor.matmul(m_ps[0:PN, n, 0:C], ones[0:PN, 0:PN], bank_sums[:, n, b, :],
                                                start=(b == 0), stop=(b == NB - 1))
                    last.then_inc(ready[layer], 1)

            batch_sums(0)

            pe.wait_ge(table_ready, 1)
            pick(0, 0)
            with pe.Fori(0, NCH // SLOTS) as i:
                for s in range(SLOTS):
                    c = i * SLOTS + s
                    pick(c + 1, (s + 1) % 2)
                    pe.wait_ge(pick_summed, c + 3)
                    pe.wait_ge(gathered[s], i * GATHERED1 + (NCH // SLOTS * GATHERED0 + GATHERED1))
                    pe.wait_ge(ea_loaded[s], i * 16 + 16)
                    pe.wait_ge(a_free, c + 1)
                    for t in range(CH):
                        last = nc.tensor.matmul(t_ps[:, s % 2, (t // SUP) * WIN:(t // SUP + 1) * WIN],
                                                rows[:, s, t, :],
                                                hot[:, bass.ds(c * CH + t, 1), :].rearrange("p a w -> p (a w)"),
                                                start=(t % SUP == 0), stop=(t % SUP == SUP - 1))
                    last.then_inc(summed, 1)

            with pe.If(flag > 0):
                with pe.Fori(0, T) as t:
                    with pe.Fori(0, NR) as r:
                        n = (t + T) * NR + r
                        pe.wait_ge(fb_fetched, (t + (T + 1)) * 16)
                        pe.wait_ge(fb_ea, t * 16 + 16)
                        pe.wait_ge(fb_w, n + 1)
                        nc.tensor.matmul(t_ps[:, 0, 0:RW], rows[:, 0, 0, :], fb_hot[:, :],
                                         start=True, stop=True).then_inc(fb_t, 1)

            pe.wait_ge(agg1_done, 2)
            for n, (a, e) in enumerate(HCH):
                if n >= 2:
                    pe.wait_ge(hid_ready, n - 1)
                nc.tensor.matmul(m_ps[:, n % 2, 0:e - a], w1[:, :], agg1[:, a:e],
                                 start=True, stop=True).then_inc(hid_ps_ready, 1)
            for b in range(NB):
                for j in bank_tiles(b):
                    pe.wait_ge(hid_ready, -(-(j + 1) * PN // MMCOL))
                    last = nc.tensor.matmul(z_ps[0:PN, b, (j % TPB) * C:(j % TPB + 1) * C],
                                            hid[:, j * PN:(j + 1) * PN], w2[:, :], start=True, stop=True)
                last.then_inc(h1_ps_ready, 1)
            batch_sums(1)

        @block.scalar
        def _(act):
            def lay_out(c, s):
                nc.scalar.copy(idx[:, s, :], src_col[:, bass.ds(c * CH, CH)]).then_inc(idx_ready, 1)

            act.wait_ge(src_col_ready, 1)
            for c in range(AHEAD):
                nc.scalar.copy(idx[:, c, :], src_col[:, c * CH:(c + 1) * CH]).then_inc(idx_ready, 1)
            for g in range(-(-NT // 4)):
                act.wait_ge(xt_turned, g + 1)
                n = min(4, NT - 4 * g) * PN
                nc.scalar.copy(xt[:, 4 * g * PN:4 * g * PN + n], t_ps[0:C, g % 2, 0:n]).then_inc(xt_ready, 1)
            act.wait_ge(xroot_done, 1)
            for b in range(NB):
                ts = bank_tiles(b)
                last = nc.scalar.copy(xroot[:, ts[0]:ts[-1] + 1, :],
                                      z_ps[0:PN, b, 0:len(ts) * C].rearrange("p (t c) -> p t c", c=C))
            last.then_inc(xroot_ready, 1)

            with act.Fori(0, NCH // SLOTS) as i:
                for s in range(SLOTS):
                    c = i * SLOTS + s
                    act.wait_ge(gathered[s], i * GATHERED0 + GATHERED0)
                    lay_out(c + AHEAD, s)
                    act.wait_ge(summed, c + (SLOTS + 1))
                    act.wait_ge(t_free, c + 1)
                    nc.scalar.copy(
                        z_sb[:, s % 2, 0:2, :, :],
                        z_ps[:, 2 * (s % 2), 0:2 * ZW].rearrange("p (w k n) -> p w k n", w=2, k=KIN))
                    nc.scalar.copy(
                        z_sb[:, s % 2, 2:4, :, :],
                        z_ps[:, 2 * (s % 2) + 1, 0:2 * ZW].rearrange("p (w k n) -> p w k n", w=2, k=KIN)
                    ).then_inc(zsb_ready, 1)
                    act.wait_ge(zsb_ready, c + 1)
                    act.sem_inc(z_free, 1)

            act.wait_ge(flag_ready, 1)
            flag = act.value_load(missed_any[0:1, 0:1], min_val=0, max_val=1 << 20)
            with act.If(flag > 0):
                with act.Fori(0, T) as t:
                    act.wait_ge(fb_added, t * NR + 1)
                    nc.scalar.copy(fb_idx[:, 0:1], src_col[:, bass.ds(t, 1)]).then_inc(fb_idx_ready, 1)
                    with act.Fori(0, NR) as r:
                        n = t * NR + r
                        act.wait_ge(fb_z, n + 1)
                        nc.scalar.copy(z_sb[:, 0, 0:2, :, :],
                                       z_ps[:, 0, 0:2 * ZW].rearrange("p (w k n) -> p w k n", w=2, k=KIN))
                        nc.scalar.copy(z_sb[:, 0, 2:4, :, :],
                                       z_ps[:, 1, 0:2 * ZW].rearrange("p (w k n) -> p w k n", w=2, k=KIN)
                                       ).then_inc(fb_zsb, 1)

            def batch_and_layer_norm(layer):
                for b in range(NB):
                    ts = bank_tiles(b)
                    act.wait_ge(centred[layer], b + 1)
                    nc.scalar.activation(sq[:, ts[0]:ts[-1] + 1, :], h[:, ts[0]:ts[-1] + 1, :],
                                         ACT.Square).then_inc(squared[layer], 1)
                act.wait_ge(var_ready[layer], 1)
                nc.scalar.activation(std[:, :], var[:, :], ACT.Sqrt).then_inc(std_ready[layer], 1)
                if layer == 0:
                    for b in range(NB):
                        ts = bank_tiles(b)
                        act.wait_ge(y_ready, b + 1)
                        nc.scalar.activation(sq[:, ts[0]:ts[-1] + 1, :], h[:, ts[0]:ts[-1] + 1, :],
                                             ACT.Exp).then_inc(exp_ready, 1)
                for b in range(NB):
                    ts = bank_tiles(b)
                    act.wait_ge(ln_centred[layer], b + 1)
                    nc.scalar.activation(sq[:, ts[0]:ts[-1] + 1, :], h[:, ts[0]:ts[-1] + 1, :],
                                         ACT.Square).then_inc(ln_squared[layer], 1)
                act.wait_ge(ln_var_ready[layer], 1)
                nc.scalar.activation(ln_std[:, :], ln_var[:, :], ACT.Sqrt).then_inc(ln_std_ready[layer], 1)

            batch_and_layer_norm(0)
            for b in range(NB):
                ts = bank_tiles(b)
                act.wait_ge(x1_ready, b + 1)
                act.dma_start(node_major(x1_dram)[:, ts[0]:ts[-1] + 1, :],
                              x1[:, ts[0]:ts[-1] + 1, :]).then_inc(x1_stored, 16)

            with act.Fori(0, NCH // SLOTS) as i:
                for s in range(SLOTS):
                    act.wait_ge(gathered[s], i * GATHERED1 + (NCH // SLOTS * GATHERED0 + GATHERED1))
                    lay_out(i * SLOTS + (s + AHEAD), s)

            with act.If(flag > 0):
                with act.Fori(0, T) as t:
                    act.wait_ge(fb_added, (t + T) * NR + 1)
                    nc.scalar.copy(fb_idx[:, 0:1], src_col[:, bass.ds(t, 1)]).then_inc(fb_idx_ready, 1)

            for n, (a, e) in enumerate(HCH):
                act.wait_ge(hid_ps_ready, n + 1)
                nc.scalar.activation(hid[:, a:e], m_ps[:, n % 2, 0:e - a], ACT.Relu,
                                     bias=b1[:, 0:1]).then_inc(hid_ready, 1)
            batch_and_layer_norm(1)

        @block.vector
        def _(dve):
            steps = [0]

            def then_wait(instruction):
                steps[0] += 1
                instruction.then_inc(dve_step, 1)
                dve.wait_ge(dve_step, steps[0])

            nc.vector.memset(src_rows[0:TB, BLK - 1, :], 0).then_inc(pads_set, 1)
            nc.vector.memset(dst_rows[0:TB, BLK - 1, :], int(NOWHERE)).then_inc(pads_set, 1)
            nc.vector.memset(ea3_rows[0:TB, BLK - 1, :, :], 0.0).then_inc(pads_set, 1)
            nc.vector.memset(ones[:, :], 1.0).then_inc(ones_ready, 1)
            nc.vector.memset(var[:, :], 0.0).then_inc(summed, SLOTS)
            nc.vector.memset(rows[:, :, :, C:P], 1.0)
            dve.wait_ge(src_loaded, 48)
            nc.vector.tensor_copy(src_rows_f[:, 0:BLK - 1, :], src_rows[:, 0:BLK - 1, :])
            nc.vector.tensor_copy(src_rows_f[0:TB, BLK - 1, :], src_rows[0:TB, BLK - 1, :]).then_inc(src_f_ready, 1)
            dve.wait_ge(dst_loaded, 48)
            nc.vector.tensor_copy(dst_rows_f[:, 0:BLK - 1, :], dst_rows[:, 0:BLK - 1, :])
            nc.vector.tensor_copy(dst_rows_f[0:TB, BLK - 1, :], dst_rows[0:TB, BLK - 1, :]).then_inc(dst_f_ready, 1)
            dve.wait_ge(src_turned, 1)
            nc.vector.tensor_copy(src_col[:, T:T + AHEAD * CH], m_ps[:, 0, 0:AHEAD * CH])
            nc.vector.tensor_copy(src_col[:, 0:T], m_ps[:, 0, 0:T]).then_inc(src_col_ready, 1)
            dve.wait_ge(dst_turned, 1)
            nc.vector.tensor_copy(base[0:1, :], m_ps[0:1, 1, 0:T:SUP])
            nc.vector.tensor_copy(dst_col[:, :], m_ps[:, 1, 0:T]).then_inc(dst_col_ready, 1)
            nc.vector.memset(basis[:, :, NK], 1.0)
            nc.vector.memset(basis[:, T:T + CH, 0:NK], 0.0)
            then_wait(nc.vector.memset(rel[:, T:T + CH], -1.0))
            dve.wait_ge(iota_ready, 1)
            nc.vector.tensor_copy(iota_f[:, :], iota_i[:, :])
            dve.wait_ge(base_spread, 1)
            dve.wait_ge(dst_col_ready, 1)
            then_wait(nc.vector.tensor_tensor(
                rel[:, 0:T].rearrange("p (g s) -> p g s", s=SUP),
                dst_col[:, :].rearrange("p (g s) -> p g s", s=SUP),
                m_ps[:, 0, 0:T // SUP].rearrange("p (g s) -> p g s", s=1).to_broadcast([P, T // SUP, SUP]),
                ALU.subtract))
            then_wait(nc.vector.tensor_scalar(real[:, :], dst_col[:, :], 0.0, None, ALU.is_ge))
            nc.vector.scalar_tensor_tensor(out=missed[:, :], in0=rel[:, 0:T], scalar=0.0, in1=real[:, :],
                                           op0=ALU.is_lt, op1=ALU.mult)
            then_wait(nc.vector.scalar_tensor_tensor(out=missed2[:, :], in0=rel[:, 0:T], scalar=float(WIN),
                                                     in1=real[:, :], op0=ALU.is_ge, op1=ALU.mult))
            then_wait(nc.vector.tensor_tensor(missed[:, :], missed[:, :], missed2[:, :], ALU.add))
            nc.vector.reduce_sum(missed_row[:, :], missed[:, :], axis=AX.X).then_inc(missed_ready, 1)
            then_wait(nc.vector.scalar_tensor_tensor(out=missed_dst[:, :], in0=dst_col[:, :], scalar=-NOWHERE,
                                                     in1=missed[:, :], op0=ALU.add, op1=ALU.mult))
            then_wait(nc.vector.tensor_scalar(missed_dst[:, :], missed_dst[:, :], NOWHERE, None, ALU.add))
            dve.wait_ge(missed_summed, 1)
            nc.vector.tensor_copy(missed_any[0:1, 0:1], m_ps[0:1, 1, 0:1]).then_inc(flag_ready, 1)
            for d in range(D):
                dve.wait_ge(ea3_turned, d + 1)
                last = nc.vector.tensor_scalar(w_lohi[:, d, :, 1], z_ps[:, d, 0:T], 0.0, 1.0, ALU.max, ALU.min)
            last.then_inc(basis_in, 1)
            dve.wait_ge(basis_in, 1)
            then_wait(nc.vector.tensor_scalar(w_lohi[:, :, :, 0], w_lohi[:, :, :, 1], -1.0, 1.0, ALU.mult, ALU.add))
            for hi in range(2):
                last = nc.vector.tensor_tensor(w_pair[:, :, 2 * hi:2 * hi + 2], w_lohi[:, 0, :, :],
                                               w_lohi[:, 1, :, hi:hi + 1].to_broadcast([P, T, 2]), ALU.mult)
            then_wait(last)
            for hi in range(2):
                last = nc.vector.tensor_tensor(basis[:, 0:T, 4 * hi:4 * hi + 4], w_pair[:, :, :],
                                               w_lohi[:, 2, :, hi:hi + 1].to_broadcast([P, T, 4]), ALU.mult)
            then_wait(last)

            def build(c, half, n, with_wait=True):
                nc.vector.tensor_tensor(
                    hot[:, bass.ds(c * CH, CH), :],
                    iota_f[:, 0:WIN].rearrange("p (a w) -> p a w", a=1).to_broadcast([P, CH, WIN]),
                    rel[:, bass.ds(c * CH, CH)].rearrange("p (t a) -> p t a", a=1).to_broadcast([P, CH, WIN]),
                    ALU.is_equal).then_inc(hot_ready, 1)
                dve.wait_ge(hot_ready, n)
                if with_wait:
                    dve.wait_ge(summed, n - 2 + SLOTS)
                nc.vector.tensor_tensor(
                    whot[:, half, :, :].rearrange("p t (k w) -> p t k w", k=KIN),
                    hot[:, bass.ds(c * CH, CH), :].rearrange("p t (a w) -> p t a w", a=1
                                                             ).to_broadcast([P, CH, KIN, WIN]),
                    basis[:, bass.ds(c * CH, CH), :].rearrange("p t (k a) -> p t k a", a=1
                                                               ).to_broadcast([P, CH, KIN, WIN]),
                    ALU.mult).then_inc(whot_ready, 1)

            nc.vector.memset(fb_rel[:, :], 0.0).then_inc(z_free, 2)
            nc.vector.memset(fb_hot[:, :], 0.0).then_inc(t_free, 2)
            nc.vector.memset(fb_whot[:, :, :, :], 0.0).then_inc(fb_added, 1)

            def windows_of(c):
                return [dve.value_load(base[0:1, bass.ds(c * WPC + w, 1)], min_val=0, max_val=N - 1)
                        for w in range(WPC)]

            def add_windows(at, c, bank, into, parts, ready, count, free, added):
                dve.wait_ge(ready, count)
                for w in range(WPC):
                    view = into[:, bass.ds(at[w], WIN)]
                    nc.vector.tensor_tensor(view, view, t_ps[0:parts, bank, w * WIN:(w + 1) * WIN],
                                            ALU.add).then_inc(added, 1)
                    dve.wait_ge(added, c * WPC + (w + 1))
                dve.sem_inc(free, 1)

            def build_pick(loads, half, picks):
                dve.wait_ge(src_wide_loaded[half], loads)
                if picks is not None:
                    dve.wait_ge(picked, picks)
                nc.vector.tensor_tensor(
                    pick_hot[:, half, :, :],
                    src_wide[:, half, :].rearrange("p (a e) -> p a e", a=1).to_broadcast([PN, NT, P]),
                    node_f[:, :].rearrange("p (t a) -> p t a", a=1).to_broadcast([PN, NT, P]),
                    ALU.is_equal).then_inc(pick_hot_ready, 1)

            def sum_pick(n, half, slot, slot_empty):
                dve.wait_ge(picked, n + 1)
                dve.wait_ge(summed, slot_empty)
                to = rows[:, slot, 0, 0:C]
                nc.vector.tensor_copy(to, m_ps[:, half, 0:C]).then_inc(part_added, 1)
                for part in range(1, SPLIT):
                    dve.wait_ge(part_added, n * (SPLIT - 1) + part)
                    nc.vector.tensor_tensor(to, to, m_ps[:, half, part * C:(part + 1) * C],
                                            ALU.add).then_inc(part_added if part < SPLIT - 1 else pick_summed, 1)

            def split_table(of):
                for part in range(SPLIT):
                    left = of if part == 0 else sq
                    if part < SPLIT - 1:
                        then_wait(nc.vector.tensor_copy(table[:, :, part, :], left[:, :, :]))
                        then_wait(nc.vector.tensor_tensor(sq[:, :, :], left[:, :, :], table[:, :, part, :],
                                                          ALU.subtract))
                    else:
                        nc.vector.tensor_copy(table[:, :, part, :], left[:, :, :]).then_inc(table_ready, 1)

            dve.wait_ge(node_ready, 1)
            then_wait(nc.vector.tensor_copy(node_f[:, :], node_i[:, :]))
            nc.vector.memset(mean[:, :], 0.0).then_inc(pick_summed, 2)
            nc.vector.memset(std[:, :], 0.0).then_inc(src_wide_free, 2)
            dve.wait_ge(aggs_zeroed, 2)
            build(0, 0, 1, False)
            with dve.Fori(0, NCH // SLOTS) as i:
                for s in range(SLOTS):
                    c = i * SLOTS + s
                    build(c + 1, (s + 1) % 2, c + 2)
                    at = windows_of(c)
                    add_windows(at, c, s % 2, agg0, C + 1, t_ready, c + 1, t_free, added0)
            nc.vector.memset(fb_rel[:, :], 0.0).then_inc(agg0_done, 1)

            def missed_ranges(t, tiles_before, weighted, into, parts):
                k0 = (t + tiles_before) * NR
                nc.vector.tensor_copy(fb_rel[:, 0:1], missed_dst[:, bass.ds(t, 1)]).then_inc(fb_step, 1)
                with dve.Fori(0, NR) as r:
                    n = k0 + r
                    dve.wait_ge(fb_step, n + t + (tiles_before + 1))
                    one_hot = nc.vector.tensor_scalar(fb_hot[:, :], iota_f[:, :], fb_rel[:, 0:1], None, ALU.is_equal)
                    one_hot.then_inc(fb_step, 1)
                    dve.wait_ge(fb_step, n + t + (tiles_before + 2))
                    if weighted:
                        for w in range(WPC):
                            last = nc.vector.tensor_tensor(
                                fb_whot[:, w, :, :],
                                fb_hot[:, w * WIN:(w + 1) * WIN].rearrange("p (a n) -> p a n", a=1
                                                                           ).to_broadcast([P, KIN, WIN]),
                                basis[:, bass.ds(t, 1), :].rearrange("p a k -> p k a").to_broadcast([P, KIN, WIN]),
                                ALU.mult)
                        last.then_inc(fb_w, 1)
                    else:
                        dve.sem_inc(fb_w, 1)
                    nc.vector.tensor_scalar(fb_rel[:, 0:1], fb_rel[:, 0:1], float(-RW), None, ALU.add)
                    dve.wait_ge(fb_t, n + 1)
                    view = into[:, bass.ds(r * RW, RW)]
                    nc.vector.tensor_tensor(view, view, t_ps[0:parts, 0, 0:RW], ALU.add).then_inc(fb_added, 1)
                    dve.wait_ge(fb_added, n + 2)

            dve.wait_ge(flag_ready, 1)
            flag = dve.value_load(missed_any[0:1, 0:1], min_val=0, max_val=1 << 20)
            with dve.If(flag > 0):
                dve.wait_ge(agg0_done, 1)
                with dve.Fori(0, T) as t:
                    missed_ranges(t, 0, True, agg0, C + 1)
            dve.wait_ge(agg0_done, 1)
            nc.vector.memset(fb_rel[:, :], 0.0).then_inc(agg0_done, 1)

            def tiles_of(a, b):
                ts = bank_tiles(b)
                return a[:, ts[0]:ts[-1] + 1, :]

            def spread(v, b):
                return v.rearrange("p (a c) -> p a c", a=1).to_broadcast([PN, len(bank_tiles(b)), C])

            def per_node(v, b):
                ts = bank_tiles(b)
                return v[:, ts[0]:ts[-1] + 1].rearrange("p (t a) -> p t a", a=1).to_broadcast([PN, len(ts), C])

            def sum_tiles(of, n, b, done):
                nc.vector.tensor_reduce(bank_sums[:, n, b, :], tiles_of(of, b).rearrange("p t c -> p c t"),
                                        AX.X, ALU.add).then_inc(done, 1)

            def batch_norm(layer, gamma, beta):
                dve.wait_ge(sums_ready[layer], 1)
                then_wait(nc.vector.tensor_scalar(mean[:, :], m_ps[0:PN, 0, 0:C], 1.0 / N, None, ALU.mult))
                for b in range(NB):
                    nc.vector.tensor_tensor(tiles_of(h, b), tiles_of(h, b), spread(mean[:, :], b),
                                            ALU.subtract).then_inc(centred[layer], 1)
                for b in range(NB):
                    dve.wait_ge(squared[layer], b + 1)
                    sum_tiles(sq, 1, b, sq_summed[layer])
                dve.wait_ge(vars_ready[layer], 1)
                nc.vector.tensor_scalar(var[:, :], m_ps[0:PN, 1, 0:C], 1.0 / N, EPS, ALU.mult, ALU.add
                                        ).then_inc(var_ready[layer], 1)
                dve.wait_ge(std_ready[layer], 1)
                then_wait(nc.vector.reciprocal(std[:, :], std[:, :]))
                then_wait(nc.vector.tensor_tensor(scale[:, :], std[:, :], gamma, ALU.mult))
                for b in range(NB):
                    last = nc.vector.tensor_tensor(tiles_of(h, b), tiles_of(h, b), spread(scale[:, :], b), ALU.mult)
                then_wait(last)
                for b in range(NB):
                    last = nc.vector.tensor_tensor(tiles_of(h, b), tiles_of(h, b), spread(beta, b), ALU.add)
                    if layer == 0:
                        last.then_inc(y_ready, 1)
                if layer == 0:
                    dve.wait_ge(y_ready, NB)
                else:
                    then_wait(last)

            def layer_norm(layer, to, ready):
                for b in range(NB):
                    ts = bank_tiles(b)
                    last = nc.vector.tensor_reduce(ln_sum[:, ts[0]:ts[-1] + 1], tiles_of(h, b), AX.X, ALU.add)
                then_wait(last)
                then_wait(nc.vector.tensor_scalar(ln_mean[:, :], ln_sum[:, :], 1.0 / C, None, ALU.mult))
                for b in range(NB):
                    nc.vector.tensor_tensor(tiles_of(h, b), tiles_of(h, b), per_node(ln_mean, b),
                                            ALU.subtract).then_inc(ln_centred[layer], 1)
                for b in range(NB):
                    ts = bank_tiles(b)
                    dve.wait_ge(ln_squared[layer], b + 1)
                    last = nc.vector.tensor_reduce(ln_sum[:, ts[0]:ts[-1] + 1], tiles_of(sq, b), AX.X, ALU.add)
                then_wait(last)
                nc.vector.tensor_scalar(ln_var[:, :], ln_sum[:, :], 1.0 / C, EPS, ALU.mult, ALU.add
                                        ).then_inc(ln_var_ready[layer], 1)
                dve.wait_ge(ln_std_ready[layer], 1)
                then_wait(nc.vector.reciprocal(ln_rstd[:, :], ln_std[:, :]))
                dve.wait_ge(ln_centred[layer], NB)
                for b in range(NB):
                    nc.vector.tensor_tensor(tiles_of(to, b), tiles_of(h, b), per_node(ln_rstd, b),
                                            ALU.mult).then_inc(ready, 1)

            dve.wait_ge(xroot_ready, 1)
            for b in range(NB):
                ts = bank_tiles(b)
                n = len(ts)
                dve.wait_ge(turned0, b + 1)
                turned = z_ps[0:PN, b, 0:n * (C + 1)].rearrange("p (t c) -> p t c", c=C + 1)
                inv = inv_cnt[:, ts[0]:ts[-1] + 1]
                then_wait(nc.vector.tensor_scalar(inv, turned[:, :, C], 1.0, None, ALU.max))
                then_wait(nc.vector.reciprocal(inv, inv))
                then_wait(nc.vector.tensor_tensor(tiles_of(h, b), turned[:, :, 0:C], per_node(inv_cnt, b), ALU.mult))
                nc.vector.tensor_tensor(tiles_of(h, b), tiles_of(h, b), tiles_of(xroot, b), ALU.add
                                        ).then_inc(h_ready[0], 1)
                dve.wait_ge(h_ready[0], b + 1)
                sum_tiles(h, 0, b, h_summed[0])
            dve.wait_ge(vecs_loaded, 80)
            batch_norm(0, vecs[:, 0, :], vecs[:, 1, :])
            for b in range(NB):
                last = nc.vector.scalar_tensor_tensor(out=tiles_of(x1, b), in0=tiles_of(h, b), scalar=0.0,
                                                      in1=tiles_of(x_nm, b), op0=ALU.max, op1=ALU.add)
            then_wait(last)
            for b in range(NB):
                dve.wait_ge(exp_ready, b + 1)
                last = nc.vector.scalar_tensor_tensor(out=tiles_of(h, b), in0=tiles_of(sq, b), scalar=1.0,
                                                      in1=tiles_of(x1, b), op0=ALU.min, op1=ALU.add)
            then_wait(last)
            layer_norm(0, x1, x1_ready)

            nc.vector.memset(fb_rel[:, :], 0.0).then_inc(a_free, 2)
            dve.wait_ge(x1_ready, NB)
            split_table(x1)
            for half in range(2):
                build_pick(16, half, None)
                dve.wait_ge(pick_hot_ready, half + 1)
                dve.sem_inc(src_wide_free, 1)
            sum_pick(0, 0, 0, NCH + 1)
            with dve.Fori(0, NCH // SLOTS) as i:
                for s in range(SLOTS):
                    c = i * SLOTS + s
                    build_pick(i * (SLOTS // 2 * 16) + (s // 2 + 2) * 16, s % 2, c + 1)
                    at = windows_of(c)
                    dve.wait_ge(pick_hot_ready, c + 3)
                    dve.sem_inc(src_wide_free, 1)
                    sum_pick(c + 1, (s + 1) % 2, (s + 1) % SLOTS, c + (NCH + 2))
                    add_windows(at, c, s % 2, agg1, P, summed, c + (NCH + SLOTS + 1), a_free, added1)
            nc.vector.memset(fb_rel[:, :], 0.0).then_inc(agg1_done, 1)
            with dve.If(flag > 0):
                dve.wait_ge(agg1_done, 1)
                with dve.Fori(0, T) as t:
                    missed_ranges(t, T, False, agg1, P)
            dve.wait_ge(agg1_done, 1)
            nc.vector.memset(fb_rel[:, :], 0.0).then_inc(agg1_done, 1)

            for b in range(NB):
                ts = bank_tiles(b)
                dve.wait_ge(h1_ps_ready, b + 1)
                nc.vector.tensor_tensor(tiles_of(h, b),
                                        z_ps[0:PN, b, 0:len(ts) * C].rearrange("p (t c) -> p t c", c=C),
                                        spread(vecs[:, 2, :], b), ALU.add).then_inc(h_ready[1], 1)
                dve.wait_ge(h_ready[1], b + 1)
                sum_tiles(h, 0, b, h_summed[1])
            batch_norm(1, vecs[:, 3, :], vecs[:, 4, :])
            for b in range(NB):
                last = nc.vector.tensor_tensor(tiles_of(h, b), tiles_of(h, b), tiles_of(x1, b), ALU.add)
            then_wait(last)
            layer_norm(1, res, out_ready)


_INS = ["x", "src", "dst", "edge_attr_3", "edge_attr_64", "L0_gnn_W", "L0_gnn_root", "L0_gnn_gamma",
        "L0_gnn_beta", "L1_gnn_W1", "L1_gnn_b1", "L1_gnn_W2", "L1_gnn_b2", "L1_gnn_bn_gamma", "L1_gnn_bn_beta"]


def kernel(**inputs):
    import numpy as np
    from concourse import bacc
    from concourse.bass_utils import run_bass_kernel_spmd

    nc = bacc.Bacc("TRN2", target_bir_lowering=False, num_devices=1)
    arrays, args = {}, []
    for name in _INS:
        a = np.ascontiguousarray(inputs[name])
        arrays[f"in_{name}"] = a
        args.append(nc.dram_tensor(f"in_{name}", a.shape, mybir.dt.from_np(a.dtype), kind="ExternalInput").ap())
    out = nc.dram_tensor("out", inputs["x"].shape, F32, kind="ExternalOutput").ap()
    gnn_two_layers(nc, *args, out)
    got = run_bass_kernel_spmd(nc, [arrays], core_ids=[0])
    return got.results[0]["out"]
```
